# Optimizing a Trainium2 kernel written in Bass

```python
import numpy as np
import jax
import jax.numpy as jnp

def _softmax(x, axis=-1):
    return jax.nn.softmax(x, axis=axis)

def _gelu(x):
    return jax.nn.gelu(x, approximate=True)

def _silu(x):
    return jax.nn.silu(x)

def _sigmoid(x):
    return jax.nn.sigmoid(x)

def _layernorm(x, axis=-1, eps=1e-05):
    m = jnp.mean(x, axis=axis, keepdims=True)
    v = jnp.var(x, axis=axis, keepdims=True)
    return (x - m) / jnp.sqrt(v + eps)

def _scatter_add(tgt, idx, src, axis=0):
    return tgt.at[idx].add(src)

def _segment_sum(src, seg, n):
    return jax.ops.segment_sum(src, seg, n)
kernel_name = 'mk_perceiver_d1_seqx_r2_772d72'

def setup_inputs(seed: int=0):
    np.random.seed(seed)
    _w = jnp.asarray

    def _rec_inputs():
        import jax
        import jax.numpy as jnp
        _rk = jax.random.key(seed)
        x = 7.22e-05 + 1 * jax.random.normal(jax.random.fold_in(_rk, 1), (16, 64, 1024), jnp.float32)
        _lenS = 64 - jax.random.randint(jax.random.fold_in(_rk, 7), (16,), 0, max(1, 64 // 4) + 1, jnp.int32)
        _lenS2 = 1601 - jax.random.randint(jax.random.fold_in(_rk, 8), (16,), 0, max(1, 1601 // 4) + 1, jnp.int32)
        _ctx_512P = jax.random.normal(jax.random.fold_in(_rk, 11), (16, 16, 256), jnp.float32)
        _ctx_512c = jax.random.dirichlet(jax.random.fold_in(_rk, 511), 0.3 * jnp.ones((16,), jnp.float32), (16, 1601))
        _ctx_512t = jnp.einsum('bsk,bkd->bsd', _ctx_512c, _ctx_512P)
        _ctx_512t = _ctx_512t * jax.lax.rsqrt(jnp.mean(jnp.square(_ctx_512t)) + 1e-12) * 0.953939
        ctx_512 = -0.000514642 + 1.00011 * (_ctx_512t + 0.3 * jax.random.normal(jax.random.fold_in(_rk, 611), (16, 1601, 256), jnp.float32))
        return (x, ctx_512)
    x, ctx_512 = _rec_inputs()

    def _L0_xattn_setup():
        import jax, jax.numpy as jnp
        import numpy as np
        B, S, H, NH, L = (2, 1024, 1024, 16, 256)
        HD = H // NH
        key = jax.random.key(seed)
        k1, k2, k3, k4, k5 = jax.random.split(key, 5)
        scale = 0.02
        return {'q': jax.random.normal(k1, (B, S, H), dtype=jnp.float32), 'latent_kv': jax.random.normal(k2, (B, S, L), dtype=jnp.float32), 'Wq': jax.random.normal(k3, (H, H), dtype=jnp.float32) * scale, 'Wkv_expand': jax.random.normal(k4, (2 * H, L), dtype=jnp.float32) * scale, 'Wout': jax.random.normal(k5, (H, H), dtype=jnp.float32) * scale}
    _L0_xattn_all = _L0_xattn_setup()
    _L0_xattn_in = {k: v for k, v in _L0_xattn_all.items() if k in ('Wq', 'Wkv_expand', 'Wout')}
    del _L0_xattn_all

    def _L0_attn_setup():
        import jax, jax.numpy as jnp
        import numpy as np
        IN_FEATURES = 1024
        HEAD_NUM = 64
        D = IN_FEATURES // HEAD_NUM
        SCALE = float(np.sqrt(D))
        key = jax.random.key(seed)
        ks = jax.random.split(key, 9)
        F = IN_FEATURES
        x = jax.random.normal(ks[0], (4, 512, F), dtype=jnp.float32)
        w = lambda k: jax.random.normal(k, (F, F), dtype=jnp.float32) * 0.02
        b = lambda k: jax.random.normal(k, (F,), dtype=jnp.float32) * 0.01
        return {'x': x, 'Wq': w(ks[1]), 'bq': b(ks[2]), 'Wk': w(ks[3]), 'bk': b(ks[4]), 'Wv': w(ks[5]), 'bv': b(ks[6]), 'Wo': w(ks[7]), 'bo': b(ks[8])}
    _L0_attn_all = _L0_attn_setup()
    _L0_attn_in = {k: v for k, v in _L0_attn_all.items() if k in ('Wq', 'bq', 'Wk', 'bk', 'Wv', 'bv', 'Wo', 'bo')}
    del _L0_attn_all

    def _L0_ffn_setup():
        import jax, jax.numpy as jnp
        import numpy as np
        key = jax.random.key(seed)
        k1, k2, k3, k4, k5 = jax.random.split(key, 5)
        B, L, H, N = (2, 1024, 1024, 4096)
        x = jax.random.normal(k1, (B, L, H), dtype=jnp.float32)
        W0 = jax.random.normal(k2, (N, H), dtype=jnp.float32) * (1.0 / np.sqrt(H))
        bias0 = jax.random.normal(k3, (N,), dtype=jnp.float32) * 0.02
        W1 = jax.random.normal(k4, (H, N), dtype=jnp.float32) * (1.0 / np.sqrt(N))
        bias1 = jax.random.normal(k5, (H,), dtype=jnp.float32) * 0.02
        return {'x': x, 'W0': W0, 'bias0': bias0, 'W1': W1, 'bias1': bias1}
    _L0_ffn_all = _L0_ffn_setup()
    _L0_ffn_in = {k: v for k, v in _L0_ffn_all.items() if k in ('W0', 'bias0', 'W1', 'bias1')}
    del _L0_ffn_all
    return {'x': x, 'ctx_512': ctx_512, 'L0_xattn_Wq': _L0_xattn_in['Wq'], 'L0_xattn_Wkv_expand': _L0_xattn_in['Wkv_expand'], 'L0_xattn_Wout': _L0_xattn_in['Wout'], 'L0_attn_Wq': _L0_attn_in['Wq'], 'L0_attn_bq': _L0_attn_in['bq'], 'L0_attn_Wk': _L0_attn_in['Wk'], 'L0_attn_bk': _L0_attn_in['bk'], 'L0_attn_Wv': _L0_attn_in['Wv'], 'L0_attn_bv': _L0_attn_in['bv'], 'L0_attn_Wo': _L0_attn_in['Wo'], 'L0_attn_bo': _L0_attn_in['bo'], 'L0_ffn_W0': _L0_ffn_in['W0'], 'L0_ffn_bias0': _L0_ffn_in['bias0'], 'L0_ffn_W1': _L0_ffn_in['W1'], 'L0_ffn_bias1': _L0_ffn_in['bias1']}

def reference(x, ctx_512, L0_xattn_Wq, L0_xattn_Wkv_expand, L0_xattn_Wout, L0_attn_Wq, L0_attn_bq, L0_attn_Wk, L0_attn_bk, L0_attn_Wv, L0_attn_bv, L0_attn_Wo, L0_attn_bo, L0_ffn_W0, L0_ffn_bias0, L0_ffn_W1, L0_ffn_bias1):
    import jax
    import jax.numpy as jnp

    def _L0_xattn_ref(q, latent_kv, Wq, Wkv_expand, Wout):
        import jax, jax.numpy as jnp
        import numpy as np
        B, S, H, NH, L = (2, 1024, 1024, 16, 256)
        HD = H // NH
        b, sq, _ = q.shape
        sk = latent_kv.shape[1]
        qp = q @ Wq.T
        kv = latent_kv @ Wkv_expand.T
        k, v = jnp.split(kv, 2, axis=-1)
        qh = qp.reshape(b, sq, NH, HD).transpose(0, 2, 1, 3)
        kh = k.reshape(b, sk, NH, HD).transpose(0, 2, 1, 3)
        vh = v.reshape(b, sk, NH, HD).transpose(0, 2, 1, 3)
        inv_sqrt_d = 1.0 / jnp.sqrt(jnp.float32(HD))
        scores = jnp.einsum('bhqd,bhkd->bhqk', qh, kh) * inv_sqrt_d
        causal = jnp.tril(jnp.ones((sq, sk), dtype=bool))
        scores = jnp.where(causal, scores, jnp.finfo(scores.dtype).min)
        attn = jax.nn.softmax(scores, axis=-1)
        out = jnp.einsum('bhqk,bhkd->bhqd', attn, vh)
        out = out.transpose(0, 2, 1, 3).reshape(b, sq, H)
        return out @ Wout.T

    def _L0_attn_ref(x, Wq, bq, Wk, bk, Wv, bv, Wo, bo):
        import jax, jax.numpy as jnp
        import numpy as np
        IN_FEATURES = 1024
        HEAD_NUM = 64
        D = IN_FEATURES // HEAD_NUM
        SCALE = float(np.sqrt(D))
        B, S, F = x.shape
        d = D
        h = F // d
        q = x @ Wq + bq
        k = x @ Wk + bk
        v = x @ Wv + bv

        def to_heads(t):
            return t.reshape(B, S, d, h).transpose(0, 2, 1, 3)
        q, k, v = (to_heads(q), to_heads(k), to_heads(v))
        scores = jnp.einsum('bdsh,bdth->bdst', q, k) / SCALE
        weights = jax.nn.softmax(scores, axis=-1)
        feats = jnp.einsum('bdst,bdth->bdsh', weights, v)
        feats = feats.transpose(0, 2, 1, 3).reshape(B, S, F)
        return feats @ Wo + bo

    def _L0_ffn_ref(x, W0, bias0, W1, bias1):
        import jax, jax.numpy as jnp
        import numpy as np
        B, L, H = x.shape
        X = x.reshape(-1, H).astype(jnp.float16)
        D = jnp.dot(X.astype(jnp.float32), W0.T) + bias0
        D = jax.nn.gelu(D, approximate=False).astype(jnp.float16)
        E = jnp.dot(D.astype(jnp.float32), W1.T) + bias1
        return E.astype(jnp.float16).reshape(B, L, H)
    x = x + _L0_xattn_ref(_layernorm(x, axis=-1), ctx_512, L0_xattn_Wq, L0_xattn_Wkv_expand, L0_xattn_Wout)
    x = x + _L0_attn_ref(_layernorm(x, axis=-1), L0_attn_Wq, L0_attn_bq, L0_attn_Wk, L0_attn_bk, L0_attn_Wv, L0_attn_bv, L0_attn_Wo, L0_attn_bo)
    x = x + _L0_ffn_ref(_layernorm(x, axis=-1), L0_ffn_W0, L0_ffn_bias0, L0_ffn_W1, L0_ffn_bias1)
    return x

_drawn_inputs = setup_inputs


def setup_inputs(seed=0):
    import zlib

    import numpy as np

    out = dict(_drawn_inputs(seed))
    spreads = {}
    factors = {'L0_xattn_Wq': 6.073,
     'L0_attn_bq': 64.0,
     'L0_attn_bk': 64.0,
     'L0_attn_bv': 8.0,
     'L0_attn_bo': 6.488,
     'L0_ffn_bias0': 5.492,
     'L0_ffn_bias1': 3.747}
    for name, (base, spread) in spreads.items():
        noise = np.random.default_rng([zlib.crc32(name.encode()), seed]).standard_normal(out[name].shape)
        drawn = base * np.exp(spread * noise) if base else spread * noise
        out[name] = jnp.asarray(drawn.astype(out[name].dtype))
    for name, factor in factors.items():
        out[name] = (out[name] * factor).astype(out[name].dtype)
    return out
```

```python
from contextlib import ExitStack

import numpy as np

import concourse.bass as bass
from concourse import mybir

F32 = mybir.dt.float32
F32R = mybir.dt.float32r
F16 = mybir.dt.float16
ALU = mybir.AluOpType
ACT = mybir.ActivationFunctionType
AX = mybir.AxisListType

P = 128
BATCHES, SEQ, HIDDEN = 16, 64, 1024
CTX = 256
FFN = 4096
HEAD_DIM = 64
LN_EPS = 1e-5
MASKED = -3.0e38

KB = HIDDEN // P
CKB = CTX // P
PAIRS = HIDDEN // (2 * HEAD_DIM)
TOKENS = BATCHES * SEQ // 2
TT = TOKENS // P
HB = BATCHES // 2
FB = FFN // P
FKB = FB // KB
SLOTS = 4

STAGES = [("cross", 0), ("cross", 1), ("self", 0), ("self", 1), ("ffn", 0), ("ffn", 1)]
ATTN_STAGES = 4

O_BANKS = [j % 3 for j in range(KB)]
O_PER_BANK = [O_BANKS.count(b) for b in range(3)]
PRODUCTS = 3 * PAIRS + KB
T_USES = 4 + PAIRS + KB // 2
FFN_TILES = FB + KB * FKB


def products_before(i):
    return PRODUCTS * min(i, ATTN_STAGES) + FFN_TILES * max(i - ATTN_STAGES, 0)


def pair_product(i, p, which):
    return products_before(i) + 3 * p + which


def o_product(i, j):
    return products_before(i) + 3 * PAIRS + j


def bank_uses_before(i, b):
    attn = min(i, ATTN_STAGES) * (PAIRS + O_PER_BANK[b])
    return attn + (max(i - ATTN_STAGES, 0) * (FB + KB) // 2 if b < 2 else 0)


def ln_uses(i):
    return T_USES * i + 4 if i >= 0 else 0


def pair_t_uses(i, p):
    return ln_uses(i) + 4 + p


def o_t_uses(i, j):
    return ln_uses(i) + 4 + PAIRS + j // 2


def ffn_t_uses(i, o):
    return ln_uses(ATTN_STAGES) + 4 + (i - ATTN_STAGES) * KB // 2 + o // 2


def o_slot(kind, j):
    return ((2, 3, 0, 1) if kind == "cross" else (3, 0, 1, 2))[j % 4]


def slot_uses_before(i, s):
    n = 0
    for k in range(i):
        kind = STAGES[k][0]
        if kind == "cross":
            n += 2 + (PAIRS if s < 2 else 0)
        elif kind == "self":
            n += 2 + (PAIRS if s < 3 else 0)
        else:
            n += FFN_TILES // SLOTS
    return n


def o_slot_use(i, j):
    kind = STAGES[i][0]
    s = o_slot(kind, j)
    in_pairs = PAIRS if s < (2 if kind == "cross" else 3) else 0
    return slot_uses_before(i, s) + in_pairs + j // 4


def build(nc, x, ctxT, xWq, xWkv, xWo, sWq, sWk, sWv, sWo, fW, bq, bk, bv, bo, b0, b1, out):
    with ExitStack() as stack:
        def sb(name, shape, dt):
            return stack.enter_context(nc.sbuf_tensor(name, shape, dt))

        def psum(name):
            return stack.enter_context(nc.psum_tensor(name, [P, 512], F32))

        def sem(name):
            return stack.enter_context(nc.semaphore(name))

        res = sb("res", [P, 2, TT, HIDDEN], F32)
        xn_hi = sb("xn_hi", [P, 2, KB, TOKENS], F32R)
        low = sb("low", [P, 4, KB, TOKENS], F32R)
        xn_lo = [low[:, 0], low[:, 3]]
        at_hi, at_lo = low[:, 1], low[:, 2]
        hidden = low[:, :].rearrange("p a k t -> p (a k) t")
        raw = sb("raw", [P, SLOTS, KB, P], F32)
        w_hi = sb("w_hi", [P, SLOTS, KB, P], F32R)
        w_lo = sb("w_lo", [P, SLOTS, KB, P], F32R)
        ctx_raw = sb("ctx_raw", [P, CKB, TOKENS], F32)
        ctx_hi = sb("ctx_hi", [P, CKB, TOKENS], F32R)
        ctx_lo = sb("ctx_lo", [P, CKB, TOKENS], F32R)
        qT = sb("qT", [P, TOKENS], F32)
        kT = sb("kT", [P, TOKENS], F32)
        vT = sb("vT", [P, TOKENS], F32)
        v_tok = sb("v_tok", [P, TT, P], F32)
        probs = sb("probs", [P, HB, SEQ], F32)
        pT = sb("pT", [P, TT, P], F32)
        o_tok = sb("o_tok", [P, TT, P], F32)
        o_T = [kT, vT]
        xn = sb("xn", [P, 2, HIDDEN], F32)
        gel = sb("gel", [P, 2, TOKENS], F16)
        e_T = sb("e_T", [P, 2, TOKENS], F16)
        ident = sb("ident", [P, P], F32)
        ident16 = sb("ident16", [P, P], F16)
        mask = sb("mask", [P, SEQ], F32)
        bq_sb, bk_sb, bv_sb, bo_sb, b1_sb = (sb(n, [P, KB], F32) for n in ("bq_sb", "bk_sb", "bv_sb", "bo_sb", "b1_sb"))
        b0_sb = sb("b0_sb", [P, FB], F32)
        stats = sb("stats", [P, TT, 2, 6], F32)
        mv = sb("mv", [P, TT, 2], F32)
        var_eps = sb("var_eps", [P, TT], F32)
        rstd = sb("rstd", [P, TT], F32)
        minus_half = sb("minus_half", [P, TT], F32)
        row_max = sb("row_max", [P, HB], F32)
        row_sum = sb("row_sum", [P, HB], F32)
        row_inv = sb("row_inv", [P, HB], F32)

        pj = [psum(f"pj{b}") for b in range(3)]
        bank_t = [psum("bank_t0"), psum("bank_t1")]
        bank_s, bank_av, bank_ot = psum("bank_s"), psum("bank_av"), psum("bank_ot")

        x_landed = [sem(f"x_landed{n}") for n in range(2 * TT)]
        ctx_landed, bias_landed = sem("ctx_landed"), sem("bias_landed")
        landed = [sem(f"landed{s}") for s in range(SLOTS)]
        hi_done = [sem(f"hi_done{s}") for s in range(SLOTS)]
        ready = [sem(f"ready{s}") for s in range(SLOTS)]
        ctx_hi_done, ctx_ready = sem("ctx_hi_done"), sem("ctx_ready")
        products = sem("products")
        pj_taken = [sem(f"pj_taken{b}") for b in range(3)]
        t_full = [sem("t_full0"), sem("t_full1")]
        t_hi = [sem("t_hi0"), sem("t_hi1")]
        t_taken = [sem("t_taken0"), sem("t_taken1")]
        s_full, s_taken = sem("s_full"), sem("s_taken")
        av_full, av_taken = sem("av_full"), sem("av_taken")
        ot_full, ot_hi, ot_taken = sem("ot_full"), sem("ot_hi"), sem("ot_taken")
        exp_done, probs_ready = sem("exp_done"), sem("probs_ready")
        soft_step, ln_step = sem("soft_step"), sem("ln_step")
        var_done, rstd_done, xn_done = sem("var_done"), sem("rstd_done"), sem("xn_done")
        gel_done, hidden_done = sem("gel_done"), sem("hidden_done")
        e_done, res_done = sem("e_done"), sem("res_done")
        const_set, const_done = sem("const_set"), sem("const_done")
        stored = sem("stored")

        START = 1

        def wait(eng, s, value):
            if not (isinstance(value, int) and value <= 0):
                eng.wait_ge(s, value)

        def pair_tiles(i):
            return [(0, 0), (1, 2)] if STAGES[i][0] == "cross" else [(0, 0), (1, 1), (2, 2)]

        def pair_source(i, p, s):
            if STAGES[i][0] == "cross":
                return (xWq, xWkv)[s][bass.ds(p, 1)]
            return (sWq, sWk, sWv)[s][bass.ds(p, 1)]

        def tile_cols(i, s, in_pairs=True):
            return 2 * CKB if in_pairs and STAGES[i][0] == "cross" and s == 1 else KB

        def refills(i):
            pass

        block = stack.enter_context(nc.Block())

        def after_pair(i, p, which):
            kind = STAGES[i][0]
            slots = {w: s for s, w in pair_tiles(i)}
            if which not in slots:
                return None
            s = slots[which]
            if isinstance(p, int) and p == PAIRS - 1:
                j = next(j for j in range(4) if o_slot(kind, j) == s)
                return o_tile(i, j)
            return s, slot_uses_before(i, s) + p + 1, pair_source(i, p + 1, s), tile_cols(i, s)

        def o_tile(i, j):
            kind = STAGES[i][0]
            return o_slot(kind, j), o_slot_use(i, j), (xWo if kind == "cross" else sWo)[j:j + 1], KB

        def early_o_tiles(i):
            return [o_tile(i, j) for j in range(2 if STAGES[i][0] == "cross" else 1)]

        def first_tile(i, s):
            if i == len(STAGES):
                return None
            if STAGES[i][0] == "ffn":
                return s, slot_uses_before(i, s), fW[s:s + 1], KB
            if s in [t[0] for t in pair_tiles(i)]:
                return s, slot_uses_before(i, s), pair_source(i, 0, s), tile_cols(i, s)
            return None

        def after_o(i, j):
            if j < 4:
                return o_tile(i, j + 4)
            return first_tile(i + 1, o_slot(STAGES[i][0], j))

        def after_ffn(i, j):
            if isinstance(j, int) and j >= FFN_TILES - 4:
                return first_tile(i + 1, j % 4)
            s = j[1] if isinstance(j, tuple) else j % 4
            at = j[0] if isinstance(j, tuple) else j
            use = slot_uses_before(i, s) + (j[2] if isinstance(j, tuple) else j // 4) + 1
            return s, use, fW[bass.ds(at + 4, 1)], KB

        @block.sync
        def _(sp):
            def load(tile):
                if tile is None:
                    return
                s, use, src, blocks = tile
                sp.wait_ge(ready[s], use + START)
                sp.dma_start(raw[:, s, 0:blocks, :], src.rearrange("a p k f -> (a p) k f")).then_inc(landed[s], 16)

            def load_x(n):
                sp.dma_start(res[:, n // TT, n % TT, :], x[n]).then_inc(x_landed[n], 16)

            load_x(0)
            load(first_tile(0, 0))
            sp.dma_start(ctx_raw[:], ctxT[0]).then_inc(ctx_landed, 16)
            for n in range(1, TT):
                load_x(n)
            load(first_tile(0, 1))
            for n in range(TT, 2 * TT):
                load_x(n)
            for i in range(ATTN_STAGES):
                for p in [0]:
                    for w in range(3):
                        load(after_pair(i, 0, w))
                    for tile in early_o_tiles(i):
                        load(tile)
                with sp.Fori(1, PAIRS - 1) as p:
                    for w in range(3):
                        load(after_pair(i, p, w))
                for w in range(3):
                    load(after_pair(i, PAIRS - 1, w))
                for j in range(KB):
                    if i == 0 and j == 0:
                        sp.wait_ge(ctx_ready, 1)
                        sp.dma_start(ctx_raw[:], ctxT[1]).then_inc(ctx_landed, 16)
                    load(after_o(i, j))
            for i in range(ATTN_STAGES, len(STAGES)):
                half = STAGES[i][1]

                def store(o, r):
                    sp.wait_ge(res_done, (i - ATTN_STAGES) * KB + r + 1)
                    for t in range(TT):
                        sp.dma_start(out[half, t, :, bass.ds(o * P, P)],
                                     res[:, half, t, bass.ds(o * P, P)]).then_inc(stored, 16)

                with sp.Fori(0, FB // 4) as g:
                    for s in range(SLOTS):
                        load(after_ffn(i, (g * 4 + s, s, g)))
                for s in range(SLOTS):
                    load(after_ffn(i, FB + s))
                with sp.Fori(1, KB - 1) as o:
                    for s in range(SLOTS):
                        load(after_ffn(i, (FB + o * 4 + s, s, FB // 4 + o)))
                    store(o - 1, o - 1)
                for s in range(SLOTS):
                    load(after_ffn(i, FFN_TILES - 4 + s))
                for o in range(KB - 2, KB):
                    store(o, o)
            sp.wait_ge(stored, 16 * 2 * KB * TT)

        @block.scalar
        def _(act):
            for n, (dst, src) in enumerate([(bq_sb, bq), (bk_sb, bk), (bv_sb, bv), (bo_sb, bo), (b1_sb, b1), (b0_sb, b0)]):
                act.dma_start(dst[:], src).then_inc(bias_landed, 16)
            act.wait_ge(bias_landed, 16 * 6)

            def round_tile(tile, freed):
                if tile is None:
                    return
                s, use, _, blocks = tile
                act.wait_ge(landed[s], 16 * (use + 1))
                wait(act, products, freed)
                nc.scalar.activation(w_hi[:, s, 0:blocks, :], raw[:, s, 0:blocks, :], ACT.Copy).then_inc(hi_done[s], 1)

            def round_ctx(n):
                act.wait_ge(ctx_landed, 16 * (n + 1))
                nc.scalar.activation(ctx_hi[:], ctx_raw[:], ACT.Copy).then_inc(ctx_hi_done, 1)

            def evacuate(dst, src, bias):
                if bias is None:
                    return nc.scalar.activation(dst, src, ACT.Copy)
                return nc.scalar.activation(dst, src, ACT.Identity, bias=bias)

            def take_pair(i, p):
                self_attn = STAGES[i][0] == "self"
                col = bass.ds(p, 1)
                wait(act, s_full, PAIRS * i + p)
                act.wait_ge(products, pair_product(i, p, 0) + 1)
                evacuate(qT[:], pj[0][:], bq_sb[:, col] if self_attn else None).then_inc(pj_taken[0], 1)
                round_tile(after_pair(i, p, 0), pair_product(i, p, 0) + 1)
                act.wait_ge(products, pair_product(i, p, 1) + 1)
                evacuate(kT[:], pj[1][:], bk_sb[:, col] if self_attn else None).then_inc(pj_taken[1], 1)
                round_tile(after_pair(i, p, 1), pair_product(i, p, 1) + 1)
                act.wait_ge(products, pair_product(i, p, 2) + 1)
                if not isinstance(p, int) or p > 0:
                    act.wait_ge(t_full[0], pair_t_uses(i, p))
                evacuate(vT[:], pj[2][:], bv_sb[:, col] if self_attn else None).then_inc(pj_taken[2], 1)
                round_tile(after_pair(i, p, 2), pair_product(i, p, 2) + 1)

            def exp_pair(i, p):
                scale = HEAD_DIM ** -0.5 if STAGES[i][0] == "cross" else 1.0 / 4.0
                act.wait_ge(s_taken, PAIRS * i + p + 1 + START)
                nc.scalar.activation(probs[:], probs[:], ACT.Exp, scale=scale).then_inc(exp_done, 1)

            def attn_hi(i, p):
                act.wait_ge(ot_full, PAIRS * i + p + 1)
                nc.scalar.activation(at_hi[:, bass.ds(p, 1), :].rearrange("p a t -> p (a t)"), bank_ot[:], ACT.Copy).then_inc(ot_hi, 1)

            def normalised(i):
                half = STAGES[i + 1][1]
                ffn = STAGES[i + 1][0] == "ffn"
                for t in range(TT):
                    for g in range(2):
                        act.wait_ge(t_full[g], ln_uses(i if i >= 0 else -1) + t + 1)
                        dst = xn_hi[:, half, 4 * g:4 * g + 4, t * P:(t + 1) * P]
                        src = bank_t[g][:, 0:256].bitcast(F16) if ffn else bank_t[g][:]
                        nc.scalar.activation(dst, src.rearrange("p (k t) -> p k t", k=4), ACT.Copy)\
                            .then_inc(t_taken[g] if ffn else t_hi[g], 1)

            round_tile(first_tile(0, 0), 0)
            round_ctx(0)
            normalised(-1)
            round_tile(first_tile(0, 1), 0)
            for i in range(ATTN_STAGES):
                take_pair(i, 0)
                normalised(i)
                for tile in early_o_tiles(i):
                    round_tile(tile, products_before(i))
                exp_pair(i, 0)
                take_pair(i, 1)
                with act.Fori(2, PAIRS - 1) as p:
                    exp_pair(i, p - 1)
                    attn_hi(i, p - 2)
                    take_pair(i, p)
                exp_pair(i, PAIRS - 2)
                attn_hi(i, PAIRS - 3)
                take_pair(i, PAIRS - 1)
                exp_pair(i, PAIRS - 1)
                attn_hi(i, PAIRS - 2)
                attn_hi(i, PAIRS - 1)
                for j in range(KB):
                    b = O_BANKS[j]
                    act.wait_ge(products, o_product(i, j) + 1)
                    act.wait_ge(t_full[j % 2], o_t_uses(i, j))
                    evacuate(o_T[j % 2][:], pj[b][:], bo_sb[:, j:j + 1] if STAGES[i][0] == "self" else None).then_inc(pj_taken[b], 1)
                    if i == 0 and j == 0:
                        round_ctx(1)
                    round_tile(after_o(i, j), o_product(i, j) + 1)
            for i in range(ATTN_STAGES, len(STAGES)):
                before = products_before(i)
                gelus = (i - ATTN_STAGES) * FB

                def gelu(j, s):
                    act.wait_ge(products, before + j + 1)
                    wait(act, hidden_done, gelus + j - 1)
                    nc.scalar.activation(gel[:, s % 2, :], pj[s % 2][:], ACT.Gelu, bias=b0_sb[:, bass.ds(j, 1)]).then_inc(gel_done, 1)

                def first_group():
                    for s in range(SLOTS):
                        gelu(s, s)
                        round_tile(after_ffn(i, s), before + s + 1)

                first_group()
                if i == ATTN_STAGES:
                    normalised(i)
                with act.Fori(1, FB // 4) as g:
                    for s in range(SLOTS):
                        gelu(g * 4 + s, s)
                        round_tile(after_ffn(i, (g * 4 + s, s, g)), g * 4 + (before + s + 1))

                def take_out(o, b, tiles):
                    for s in range(SLOTS):
                        act.wait_ge(products, o * 4 + (before + FB + s + 1))
                        if s == SLOTS - 1:
                            act.wait_ge(t_full[b], ffn_t_uses(i, 0) + o_half(o, b))
                            nc.scalar.activation(e_T[:, b, :], pj[b][:], ACT.Identity, bias=b1_sb[:, bass.ds(o, 1)]).then_inc(e_done, 1)
                        round_tile(tiles[s], o * 4 + (before + FB + s + 1))

                with act.Fori(0, KB // 2 - 1) as g:
                    for b in range(2):
                        def o_half(o, b, g=g):
                            return g
                        take_out(g * 2 + b, b, [after_ffn(i, (g * 8 + (FB + 4 * b + s), s, g * 2 + (FB // 4 + b))) for s in range(SLOTS)])
                for o in range(KB - 2, KB):
                    def o_half(o, b):
                        return o // 2
                    take_out(o, o % 2, [after_ffn(i, FB + 4 * o + s) for s in range(SLOTS)])

        def lower(engine, eng, tile):
            if tile is None:
                return
            s, use, _, blocks = tile
            eng.wait_ge(hi_done[s], use + 1)
            engine.tensor_tensor(w_lo[:, s, 0:blocks, :], raw[:, s, 0:blocks, :], w_hi[:, s, 0:blocks, :].bitcast(F32),
                                 ALU.subtract).then_inc(ready[s], 1)

        @block.gpsimd
        def _(pool):
            nc.gpsimd.memset(minus_half[:], -0.5).then_inc(const_set, 1)
            nc.gpsimd.memset(ident[:], 0.0).then_inc(const_set, 1)
            nc.gpsimd.memset(mask[:], 0.0).then_inc(const_set, 1)
            pool.wait_ge(const_set, 3)
            nc.gpsimd.affine_select(out=ident[:], in_=ident[:], compare_op=ALU.not_equal, fill=1.0, base=0,
                                    pattern=[[-1, P]], channel_multiplier=1).then_inc(const_set, 1)
            pool.wait_ge(const_set, 4)
            nc.gpsimd.tensor_copy(ident16[:], ident[:]).then_inc(const_done, 1)

            def lower_ctx(n):
                pool.wait_ge(ctx_hi_done, n + 1)
                nc.gpsimd.tensor_tensor(ctx_lo[:], ctx_raw[:], ctx_hi[:].bitcast(F32), ALU.subtract).then_inc(ctx_ready, 1)

            def inverse_root(n):
                pool.wait_ge(var_done, n + 1)
                nc.gpsimd.tensor_tensor(rstd[:], var_eps[:], minus_half[:], ALU.pow).then_inc(rstd_done, 1)

            lower(nc.gpsimd, pool, first_tile(0, 0))
            inverse_root(0)
            pool.wait_ge(rstd_done, 1)
            for h in range(2):
                part = slice(SEQ * h, SEQ * (h + 1))
                pool.wait_ge(const_done, 1 + h)
                nc.gpsimd.affine_select(out=mask[part], in_=mask[part], compare_op=ALU.is_ge, fill=MASKED, base=0,
                                        pattern=[[-1, SEQ]], channel_multiplier=1).then_inc(const_done, 1)
            pool.wait_ge(const_done, 3)
            lower_ctx(0)
            lower(nc.gpsimd, pool, first_tile(0, 1))
            for i in range(ATTN_STAGES):
                inverse_root(i + 1)
                for w in range(3):
                    lower(nc.gpsimd, pool, after_pair(i, 0, w))
                for tile in early_o_tiles(i):
                    lower(nc.gpsimd, pool, tile)
                with pool.Fori(1, PAIRS - 1) as p:
                    for w in range(3):
                        lower(nc.gpsimd, pool, after_pair(i, p, w))
                for w in range(3):
                    lower(nc.gpsimd, pool, after_pair(i, PAIRS - 1, w))
                for j in range(KB):
                    if i == 0 and j == 0:
                        lower_ctx(1)
                    lower(nc.gpsimd, pool, after_o(i, j))
            inverse_root(ATTN_STAGES + 1)

        @block.vector
        def _(dve):
            ln_steps = 0

            def statistics(n, half):
                nonlocal ln_steps
                for t in range(TT):
                    if n < 2:
                        dve.wait_ge(x_landed[half * TT + t], 16)
                    for g in range(2):
                        last = nc.vector.bn_stats(stats[:, t, g, :], res[:, half, t, g * 512:(g + 1) * 512])
                last.then_inc(ln_step, 1)
                ln_steps += 1
                dve.wait_ge(ln_step, ln_steps)
                for t in range(TT):
                    last = nc.vector.bn_aggr(mv[:, t, :], stats[:, t, :, :].rearrange("p g s -> p (g s)"))
                last.then_inc(ln_step, 1)
                ln_steps += 1
                dve.wait_ge(ln_step, ln_steps)
                nc.vector.tensor_scalar(var_eps[:], mv[:, :, 1], LN_EPS, None, ALU.add).then_inc(var_done, 1)

            def normalise(i):
                kind, half = STAGES[i + 1]
                ffn = kind == "ffn"
                n = i + 1
                uses = ln_uses(i)
                statistics(n, half)
                dve.wait_ge(rstd_done, n + 1)

                def one(t):
                    dst = xn[:, t % 2, 0:HIDDEN // 2].bitcast(F16) if ffn else xn[:, t % 2, :]
                    wait(dve, t_full[1], uses + t - 1 if t >= 2 else (uses if i >= 0 else 0))
                    nc.vector.tensor_scalar(dst, res[:, half, t, :], mv[:, t, 0:1], rstd[:, t:t + 1],
                                            ALU.subtract, ALU.mult).then_inc(xn_done, 1)

                def rest(t):
                    if ffn:
                        return
                    for g in range(2):
                        hi_count = hi_uses(i, t)
                        dve.wait_ge(t_hi[g], hi_count)
                        cols = (slice(None), slice(4 * g, 4 * g + 4), slice(t * P, (t + 1) * P))
                        nc.vector.tensor_tensor(xn_lo[half][cols], bank_t[g][:].rearrange("p (k t) -> p k t", k=4),
                                                xn_hi[:, half][cols].bitcast(F32), ALU.subtract).then_inc(t_taken[g], 1)

                one(0)
                one(1)
                for t in range(TT):
                    rest(t)
                    if t + 2 < TT:
                        one(t + 2)

            def hi_uses(i, t):
                return TT * (i + 1) + t + 1

            def by_batch(ap):
                return ap.unsqueeze(2).to_broadcast([P, HB, SEQ])

            def softmax(i, p):
                self_attn = STAGES[i][0] == "self"
                n = PAIRS * i + p
                t_uses = pair_t_uses(i, p)
                scores = bank_s[:].rearrange("p (b k) -> p b k", b=HB)
                dve.wait_ge(s_full, n + 1)
                dve.wait_ge(t_full[1], t_uses)
                if not self_attn:
                    if isinstance(n, int) and n == 0:
                        dve.wait_ge(const_done, 3)
                    nc.vector.tensor_tensor(probs[:], scores, mask[:].unsqueeze(1).to_broadcast([P, HB, SEQ]),
                                            ALU.add).then_inc(soft_step, 1)
                    dve.wait_ge(soft_step, soft_steps(i, p, 1))
                    scores = probs[:]
                k = 0 if self_attn else 1
                nc.vector.tensor_reduce(row_max[:], scores, AX.X, ALU.max).then_inc(soft_step, 1)
                dve.wait_ge(soft_step, soft_steps(i, p, k + 1))
                nc.vector.tensor_tensor(probs[:], scores, by_batch(row_max[:]), ALU.subtract).then_inc(s_taken, 1)
                dve.wait_ge(exp_done, n + 1)
                nc.vector.tensor_reduce(row_sum[:], probs[:], AX.X, ALU.add).then_inc(soft_step, 1)
                dve.wait_ge(soft_step, soft_steps(i, p, k + 2))
                nc.vector.reciprocal(row_inv[:], row_sum[:]).then_inc(soft_step, 1)
                dve.wait_ge(soft_step, soft_steps(i, p, k + 3))
                nc.vector.tensor_tensor(probs[:], probs[:], by_batch(row_inv[:]), ALU.mult).then_inc(probs_ready, 1)

            def values(i, p):
                n = PAIRS * i + p
                t_uses = pair_t_uses(i, p)
                dve.wait_ge(t_full[0], t_uses + 1)
                wait(dve, av_full, n)
                nc.vector.tensor_copy(v_tok[:].rearrange("p t d -> p (t d)"), bank_t[0][:]).then_inc(t_taken[0], 1)
                dve.wait_ge(t_full[1], t_uses + 1)
                nc.vector.tensor_copy(pT[:].rearrange("p t q -> p (t q)"), bank_t[1][:]).then_inc(t_taken[1], 1)
                dve.wait_ge(av_full, n + 1)
                wait(dve, ot_full, n)
                nc.vector.tensor_copy(o_tok[:].rearrange("p t d -> p (t d)"), bank_av[:]).then_inc(av_taken, 1)

            def attn_lo(i, p):
                dve.wait_ge(ot_hi, PAIRS * i + p + 1)
                at = bass.ds(p, 1)
                nc.vector.tensor_tensor(at_lo[:, at, :].rearrange("p a t -> p (a t)"), bank_ot[:],
                                        at_hi[:, at, :].rearrange("p a t -> p (a t)").bitcast(F32), ALU.subtract).then_inc(ot_taken, 1)

            def soft_steps(i, p, k):
                per = {"cross": 4, "self": 3}
                before = sum(per[STAGES[n][0]] * PAIRS for n in range(i))
                return p * per[STAGES[i][0]] + (before + k)

            normalise(-1)
            for i in range(ATTN_STAGES):
                half = STAGES[i][1]
                normalise(i)
                softmax(i, 0)
                values(i, 0)
                with dve.Fori(1, PAIRS) as p:
                    softmax(i, p)
                    attn_lo(i, p - 1)
                    values(i, p)
                attn_lo(i, PAIRS - 1)
                for j in range(KB):
                    g = j % 2
                    dve.wait_ge(t_full[g], o_t_uses(i, j) + 1)
                    here = res[:, half, :, j * P:(j + 1) * P]
                    nc.vector.tensor_tensor(here, here, bank_t[g][:].rearrange("p (t f) -> p t f", t=TT),
                                            ALU.add).then_inc(t_taken[g], 1)
                for g in range(2):
                    dve.wait_ge(t_taken[g], o_t_uses(i, KB - 1) + 1)
            for i in range(ATTN_STAGES, len(STAGES)):
                half = STAGES[i][1]
                gelus = (i - ATTN_STAGES) * FB

                def copy_hidden(j, s):
                    dve.wait_ge(gel_done, gelus + j + 1)
                    nc.vector.tensor_copy(hidden[:, bass.ds(j, 1), :].rearrange("p a t -> p (a t)"), gel[:, s % 2, :]).then_inc(hidden_done, 1)

                for s in range(SLOTS):
                    copy_hidden(s, s)
                    lower(nc.vector, dve, after_ffn(i, s))
                if i == ATTN_STAGES:
                    normalise(i)
                with dve.Fori(1, FB // 4) as g:
                    for s in range(SLOTS):
                        copy_hidden(g * 4 + s, s)
                        lower(nc.vector, dve, after_ffn(i, (g * 4 + s, s, g)))

                def add_out(o, b, half_o):
                    dve.wait_ge(t_full[b], half_o + (ffn_t_uses(i, 0) + 1))
                    here = res[:, half, :, bass.ds(o * P, P)]
                    nc.vector.tensor_tensor(here, here, bank_t[b][:, 0:256].bitcast(F16).rearrange("p (t f) -> p t f", t=TT),
                                            ALU.add).then_inc(res_done, 1)

                def out_step(o, tiles, add):
                    for s in range(SLOTS):
                        lower(nc.vector, dve, tiles[s])
                        if s == 1 and add:
                            add_out(*add)

                def later_tiles(g, b):
                    return [after_ffn(i, (g * 8 + (FB + 4 * b + s), s, g * 2 + (FB // 4 + b))) for s in range(SLOTS)]

                out_step(0, [after_ffn(i, FB + s) for s in range(SLOTS)], None)
                out_step(1, [after_ffn(i, FB + 4 + s) for s in range(SLOTS)], (0, 0, 0))
                with dve.Fori(1, KB // 2 - 1) as g:
                    out_step(g * 2, later_tiles(g, 0), (g * 2 - 1, 1, g - 1))
                    out_step(g * 2 + 1, later_tiles(g, 1), (g * 2, 0, g))
                for o in range(KB - 2, KB):
                    out_step(o, [after_ffn(i, FB + 4 * o + s) for s in range(SLOTS)], (o - 1, (o - 1) % 2, (o - 1) // 2))
                add_out(KB - 1, 1, KB // 2 - 1)

        @block.tensor
        def _(pe):
            for s in [*ready, *pj_taken, s_taken, av_taken, ot_taken]:
                pe.sem_inc(s, START)
            pe.wait_ge(const_done, 1)

            def accumulate(bank, terms, start=True, stop=True):
                for n, (lhs, rhs) in enumerate(terms):
                    last = nc.tensor.matmul(bank[:], lhs, rhs, start=start and n == 0, stop=stop and n == len(terms) - 1)
                return last

            def exact(s, blocks, hi, lo):
                for n, k in enumerate(blocks):
                    yield w_hi[:, s, k, :], hi[:, n, :]
                    yield w_hi[:, s, k, :], lo[:, n, :]
                    yield w_lo[:, s, k, :], hi[:, n, :]

            def tile_ready(s, use):
                pe.wait_ge(ready[s], use + 1 + START)

            def project(i, p, which, *between):
                kind, half = STAGES[i]
                pe.wait_ge(pj_taken[which], bank_uses_before(i, which) + p + START)
                s = which if kind == "self" else min(which, 1)
                if which == 0 or kind == "self" or which == 1:
                    tile_ready(s, slot_uses_before(i, s) + p)
                if kind == "cross" and which:
                    blocks, hi, lo = range(CKB * (which - 1), CKB * which), ctx_hi, ctx_lo
                else:
                    blocks, hi, lo = range(KB), xn_hi[:, half], xn_lo[half]
                cuts = [0, *(block for block, _ in between), len(blocks)]
                for n, (first, end) in enumerate(zip(cuts, cuts[1:])):
                    if n:
                        between[n - 1][1]()
                    if first < end:
                        terms = list(exact(s, blocks[first:end], hi[:, first:end], lo[:, first:end]))
                        last = accumulate(pj[which], terms, start=first == 0, stop=end == len(blocks))
                last.then_inc(products, 1)

            def scores_inputs(i, p):
                n = PAIRS * i + p
                pe.wait_ge(pj_taken[0], bank_uses_before(i, 0) + p + 1 + START)
                pe.wait_ge(pj_taken[1], bank_uses_before(i, 1) + p + 1 + START)
                pe.wait_ge(s_taken, n + START)

            def scores():
                for b in range(HB):
                    cols = slice(SEQ * b, SEQ * (b + 1))
                    for h in range(2):
                        head = slice(HEAD_DIM * h, HEAD_DIM * (h + 1))
                        last = nc.tensor.matmul(bank_s[head, cols], qT[head, cols], kT[head, cols], start=True, stop=True)
                last.then_inc(s_full, 1)

            def transpose_v(i, p):
                pe.wait_ge(pj_taken[2], bank_uses_before(i, 2) + p + 1 + START)
                pe.wait_ge(t_taken[0], pair_t_uses(i, p))
                for t in range(TT):
                    cols = slice(t * P, (t + 1) * P)
                    last = nc.tensor.transpose(bank_t[0][:, cols], vT[:, cols], ident[:])
                last.then_inc(t_full[0], 1)

            def transpose_probs(i, p):
                pe.wait_ge(probs_ready, PAIRS * i + p + 1)
                pe.wait_ge(t_taken[1], pair_t_uses(i, p))
                flat = probs[:].rearrange("p b k -> p (b k)")
                for t in range(TT):
                    cols = slice(t * P, (t + 1) * P)
                    last = nc.tensor.transpose(bank_t[1][:, cols], flat[:, cols], ident[:])
                last.then_inc(t_full[1], 1)

            def values_inputs(i, p):
                pe.wait_ge(t_taken[0], pair_t_uses(i, p) + 1)
                pe.wait_ge(t_taken[1], pair_t_uses(i, p) + 1)
                pe.wait_ge(av_taken, PAIRS * i + p + START)

            def weigh_values():
                for t in range(TT):
                    for h in range(2):
                        head = slice(HEAD_DIM * h, HEAD_DIM * (h + 1))
                        for b in range(2):
                            rows = slice(SEQ * b, SEQ * (b + 1))
                            last = nc.tensor.matmul(bank_av[rows, t * P + HEAD_DIM * h:t * P + HEAD_DIM * (h + 1)],
                                                    pT[rows, t, head], v_tok[rows, t, head], start=True, stop=True)
                last.then_inc(av_full, 1)

            def transpose_out(i, p):
                pe.wait_ge(av_taken, PAIRS * i + p + 1 + START)
                pe.wait_ge(ot_taken, PAIRS * i + p + START)
                for t in range(TT):
                    last = nc.tensor.transpose(bank_ot[:, t * P:(t + 1) * P], o_tok[:, t, :], ident[:])
                last.then_inc(ot_full, 1)

            def normalised(i):
                ffn = STAGES[i + 1][0] == "ffn"
                for t in range(TT):
                    pe.wait_ge(xn_done, TT * (i + 1) + t + 1)
                    for g in range(2):
                        wait(pe, t_taken[g], ln_uses(i) + t)
                        for k in range(4):
                            cols = slice((4 * g + k) * P, (4 * g + k + 1) * P)
                            if ffn:
                                last = nc.tensor.transpose(bank_t[g][:, 0:256].bitcast(F16)[:, k * P:(k + 1) * P],
                                                           xn[:, t % 2, 0:HIDDEN // 2].bitcast(F16)[:, cols], ident16[:])
                            else:
                                last = nc.tensor.transpose(bank_t[g][:, k * P:(k + 1) * P], xn[:, t % 2, cols], ident[:])
                        last.then_inc(t_full[g], 1)

            def xn_is_ready(i):
                for g in range(2):
                    pe.wait_ge(t_taken[g], ln_uses(i - 1) + 4)

            normalised(-1)
            for i in range(ATTN_STAGES):
                kind, half = STAGES[i]
                xn_is_ready(i)
                if kind == "cross":
                    project(i, 0, 0)
                    pe.wait_ge(ctx_ready, i + 1)
                    project(i, 0, 1)
                    project(i, 0, 2)
                else:
                    for which in range(3):
                        project(i, 0, which)
                normalised(i)
                v_blocks = CKB if kind == "cross" else KB

                def pair_step(p, out_before):
                    scores_inputs(i, p - 1)
                    if out_before:
                        project(i, p, 0, (1, scores), (KB // 2, lambda: transpose_out(i, p - 2)))
                    else:
                        project(i, p, 0, (1, scores))
                    transpose_v(i, p - 1)
                    project(i, p, 1)
                    transpose_probs(i, p - 1)
                    project(i, p, 2, (v_blocks - 1, lambda: values_inputs(i, p - 1)))
                    weigh_values()

                pair_step(1, False)
                with pe.Fori(2, PAIRS) as p:
                    pair_step(p, True)

                last = PAIRS - 1

                def o_part(j, blocks, start, stop):
                    s, b = o_slot(kind, j), O_BANKS[j]
                    if start:
                        pe.wait_ge(pj_taken[b], bank_uses_before(i, b) + PAIRS + j // 3 + START)
                        tile_ready(s, o_slot_use(i, j))
                    terms = list(exact(s, blocks, at_hi[:, blocks.start:blocks.stop], at_lo[:, blocks.start:blocks.stop]))
                    return accumulate(pj[b], terms, start, stop)

                def open_tiles(*parts):
                    for j, first, end in parts:
                        o_part(j, range(first, end), first == 0, False)

                scores_inputs(i, last)
                scores()
                pe.wait_ge(ot_taken, PAIRS * i + last - 1 + START)
                open_tiles((0, 0, 4))
                transpose_out(i, last - 1)
                open_tiles((0, 4, 6))
                transpose_v(i, last)
                open_tiles((1, 0, 6))
                transpose_probs(i, last)
                pe.wait_ge(ot_taken, PAIRS * i + last + START)
                open_tiles((0, 6, 7), (1, 6, 7))
                values_inputs(i, last)
                weigh_values()
                open_tiles((2, 0, 4))
                transpose_out(i, last)
                open_tiles((2, 4, 7))
                pe.wait_ge(ot_taken, PAIRS * i + last + 1 + START)

                def transpose_o(j):
                    g, b = j % 2, O_BANKS[j]
                    pe.wait_ge(pj_taken[b], bank_uses_before(i, b) + PAIRS + j // 3 + 1 + START)
                    pe.wait_ge(t_taken[g], o_t_uses(i, j))
                    for t in range(TT):
                        cols = slice(t * P, (t + 1) * P)
                        done = nc.tensor.transpose(bank_t[g][:, cols], o_T[g][:, cols], ident[:])
                    done.then_inc(t_full[g], 1)

                for j in range(KB):
                    if j < 3:
                        o_part(j, range(KB - 1, KB), False, True).then_inc(products, 1)
                    else:
                        o_part(j, range(0, KB), True, True).then_inc(products, 1)
                    if j:
                        transpose_o(j - 1)
                transpose_o(KB - 1)

            for i in range(ATTN_STAGES, len(STAGES)):
                half = STAGES[i][1]
                n = i - ATTN_STAGES
                bank_base = bank_uses_before(i, 0)
                xn_is_ready(i if i == ATTN_STAGES else ATTN_STAGES + 1)

                def ffn_up(g):
                    for s in range(SLOTS):
                        b = s % 2
                        if s >= 2:
                            pe.wait_ge(gel_done, g * 4 + (n * FB + s - 1))
                        elif isinstance(g, int):
                            if n == 0:
                                pe.wait_ge(pj_taken[b], bank_base + START)
                            else:
                                pe.wait_ge(e_done, n * KB)
                        else:
                            pe.wait_ge(gel_done, g * 4 + (n * FB + s - 1))
                        tile_ready(s, slot_uses_before(i, s) + g)
                        terms = [(w[:, s, k, :], xn_hi[:, half, k, :]) for k in range(KB) for w in (w_hi, w_lo)]
                        accumulate(pj[b], terms).then_inc(products, 1)

                def ffn_down(o, b, before=None):
                    if isinstance(o, int) and o < 2:
                        pe.wait_ge(gel_done, (n + 1) * FB)
                        pe.wait_ge(hidden_done, (n + 1) * FB)
                    else:
                        pe.wait_ge(e_done, o + (n * KB - 1))
                    for s in range(SLOTS):
                        tile_ready(s, o + (slot_uses_before(i, s) + FB // 4))
                        terms = [(w[:, s, k, :], hidden[:, s * KB + k, :]) for k in range(KB) for w in (w_hi, w_lo)]
                        accumulate(pj[b], terms, start=s == 0, stop=s == SLOTS - 1).then_inc(products, 1)
                        if s == 0 and before is not None:
                            transpose_e(before, 1 - b)

                def transpose_e(o, b):
                    pe.wait_ge(e_done, o + (n * KB + 1))
                    if isinstance(o, int) and n * KB + o < 2:
                        pe.wait_ge(t_taken[b], ffn_t_uses(i, o))
                    else:
                        pe.wait_ge(res_done, o + (n * KB - 1))
                    bank16 = bank_t[b][:, 0:256].bitcast(F16)
                    for t in range(TT):
                        cols = slice(t * P, (t + 1) * P)
                        done = nc.tensor.transpose(bank16[:, cols], e_T[:, b, cols], ident16[:])
                    done.then_inc(t_full[b], 1)

                ffn_up(0)
                if i == ATTN_STAGES:
                    normalised(i)
                with pe.Fori(1, FB // 4) as g:
                    ffn_up(g)
                ffn_down(0, 0)
                ffn_down(1, 1, 0)
                with pe.Fori(1, KB // 2) as g:
                    ffn_down(g * 2, 0, g * 2 - 1)
                    ffn_down(g * 2 + 1, 1, g * 2)
                transpose_e(KB - 1, 1)


def weight_tiles(w, out_blocks, in_blocks):
    return w.reshape(out_blocks, P, in_blocks, P).transpose(0, 3, 2, 1)


def kernel(x, ctx_512, L0_xattn_Wq, L0_xattn_Wkv_expand, L0_xattn_Wout, L0_attn_Wq, L0_attn_bq, L0_attn_Wk,
           L0_attn_bk, L0_attn_Wv, L0_attn_bv, L0_attn_Wo, L0_attn_bo, L0_ffn_W0, L0_ffn_bias0, L0_ffn_W1,
           L0_ffn_bias1):
    from concourse import bacc
    from concourse.bass_utils import run_bass_kernel_spmd

    def columns(b):
        return np.asarray(b).reshape(-1, P).T

    wkv = np.asarray(L0_xattn_Wkv_expand)
    kv = [weight_tiles(wkv[n * HIDDEN:(n + 1) * HIDDEN], PAIRS, CKB) for n in range(2)]
    ctx = np.asarray(ctx_512)[:, :SEQ, :].reshape(2, TOKENS, CKB, P).transpose(0, 3, 2, 1)
    w1 = np.asarray(L0_ffn_W1).reshape(KB, P, FKB, KB, P).transpose(0, 2, 4, 3, 1).reshape(KB * FKB, P, KB, P)
    ins = {
        "x": np.asarray(x).reshape(2 * TT, P, HIDDEN),
        "ctxT": ctx,
        "xWq": weight_tiles(np.asarray(L0_xattn_Wq), PAIRS, KB),
        "xWkv": np.concatenate(kv, axis=2),
        "xWo": weight_tiles(np.asarray(L0_xattn_Wout), KB, KB),
        "sWq": weight_tiles(np.asarray(L0_attn_Wq).T, PAIRS, KB),
        "sWk": weight_tiles(np.asarray(L0_attn_Wk).T, PAIRS, KB),
        "sWv": weight_tiles(np.asarray(L0_attn_Wv).T, PAIRS, KB),
        "sWo": weight_tiles(np.asarray(L0_attn_Wo).T, KB, KB),
        "fW": np.concatenate([weight_tiles(np.asarray(L0_ffn_W0), FB, KB), w1], axis=0),
        "bq": columns(L0_attn_bq), "bk": columns(L0_attn_bk), "bv": columns(L0_attn_bv),
        "bo": columns(L0_attn_bo), "b0": columns(L0_ffn_bias0), "b1": columns(L0_ffn_bias1),
    }
    ins = {f"in_{n}": np.ascontiguousarray(a) for n, a in ins.items()}
    nc = bacc.Bacc("TRN2", target_bir_lowering=False, num_devices=1, dynamic_dma_scratch_size=1024)
    args = [nc.dram_tensor(n, a.shape, F32, kind="ExternalInput").ap() for n, a in ins.items()]
    out = nc.dram_tensor("out", (2, TT, P, HIDDEN), F32, kind="ExternalOutput").ap()
    build(nc, *args, out)
    result = run_bass_kernel_spmd(nc, [ins], core_ids=[0])
    return result.results[0]["out"].reshape(BATCHES, SEQ, HIDDEN)
```

```python
from contextlib import ExitStack

import numpy as np

import concourse.bass as bass
from concourse import mybir

F32 = mybir.dt.float32
F32R = mybir.dt.float32r
F16 = mybir.dt.float16
ALU = mybir.AluOpType
ACT = mybir.ActivationFunctionType
AX = mybir.AxisListType

P = 128
BATCHES, SEQ, HIDDEN = 16, 64, 1024
CTX = 256
FFN = 4096
HEAD_DIM = 64
LN_EPS = 1e-5
MASKED = -3.0e38

KB = HIDDEN // P
CKB = CTX // P
PAIRS = HIDDEN // (2 * HEAD_DIM)
TOKENS = BATCHES * SEQ // 2
TT = TOKENS // P
HB = BATCHES // 2
FB = FFN // P
FKB = FB // KB
SLOTS = 4

STAGES = [("cross", 0), ("cross", 1), ("self", 0), ("self", 1), ("ffn", 0), ("ffn", 1)]
ATTN_STAGES = 4

O_BANKS = [j % 3 for j in range(KB)]
O_PER_BANK = [O_BANKS.count(b) for b in range(3)]
PRODUCTS = 3 * PAIRS + KB
T_USES = PAIRS + KB // 2
FFN_TILES = FB + KB * FKB


def products_before(i):
    return PRODUCTS * min(i, ATTN_STAGES) + FFN_TILES * max(i - ATTN_STAGES, 0)


def pair_product(i, p, which):
    return products_before(i) + 3 * p + which


def o_product(i, j):
    return products_before(i) + 3 * PAIRS + j


def bank_uses_before(i, b):
    attn = min(i, ATTN_STAGES) * (PAIRS + O_PER_BANK[b])
    return attn + (max(i - ATTN_STAGES, 0) * (FB + KB) // 2 if b < 2 else 0)


def pair_t_uses(i, p):
    return T_USES * i + p


def o_t_uses(i, j):
    return T_USES * i + PAIRS + j // 2


def ffn_t_uses(i, o):
    return T_USES * ATTN_STAGES + (i - ATTN_STAGES) * KB // 2 + o // 2


def ln_tiles(n, t):
    return TT * n + t


def o_slot(kind, j):
    return ((2, 3, 0, 1) if kind == "cross" else (3, 0, 1, 2))[j % 4]


def slot_uses_before(i, s):
    n = 0
    for k in range(i):
        kind = STAGES[k][0]
        if kind == "cross":
            n += 2 + (PAIRS if s < 2 else 0)
        elif kind == "self":
            n += 2 + (PAIRS if s < 3 else 0)
        else:
            n += FFN_TILES // SLOTS
    return n


def o_slot_use(i, j):
    kind = STAGES[i][0]
    s = o_slot(kind, j)
    in_pairs = PAIRS if s < (2 if kind == "cross" else 3) else 0
    return slot_uses_before(i, s) + in_pairs + j // 4


def build(nc, x, ctxT, xWq, xWkv, xWo, sWq, sWk, sWv, sWo, fW, bq, bk, bv, bo, b0, b1, out):
    with ExitStack() as stack:
        def sb(name, shape, dt):
            return stack.enter_context(nc.sbuf_tensor(name, shape, dt))

        def psum(name, cols=512):
            return stack.enter_context(nc.psum_tensor(name, [P, cols], F32))

        def sem(name):
            return stack.enter_context(nc.semaphore(name))

        res = sb("res", [P, 2, TT, HIDDEN], F32)
        xn_hi = sb("xn_hi", [P, 2, KB, TOKENS], F32R)
        low = sb("low", [P, 4, KB, TOKENS], F32R)
        xn_lo = [low[:, 0], low[:, 3]]
        at_hi, at_lo = low[:, 1], low[:, 2]
        hidden = low[:, :].rearrange("p a k t -> p (a k) t")
        raw = sb("raw", [P, SLOTS, KB, P], F32)
        w_hi = sb("w_hi", [P, SLOTS, KB, P], F32R)
        w_lo = sb("w_lo", [P, SLOTS, KB, P], F32R)
        ctx_raw = sb("ctx_raw", [P, CKB, TOKENS], F32)
        ctx_hi = sb("ctx_hi", [P, CKB, TOKENS], F32R)
        ctx_lo = sb("ctx_lo", [P, CKB, TOKENS], F32R)
        qT = sb("qT", [P, TOKENS], F32)
        kT = sb("kT", [P, TOKENS], F32)
        vT = sb("vT", [P, TOKENS], F32)
        v_hi = sb("v_hi", [P, TT, P], F32R)
        v_lo = sb("v_lo", [P, TT, P], F32R)
        probs = sb("probs", [P, HB, SEQ], F32)
        pd_hi = sb("pd_hi", [P, TT, 2, 2, SEQ], F32R)
        pd_lo = sb("pd_lo", [P, TT, 2, 2, SEQ], F32R)
        o_T = [kT, vT]
        xn = sb("xn", [P, 2, HIDDEN], F32)
        ffn_tiles = xn[:].rearrange("p a f -> p (a f)").bitcast(F16).rearrange("p (t f) -> p t f", t=TT)
        gel = sb("gel", [P, 2, TOKENS], F16)
        e_T = sb("e_T", [P, 2, TOKENS], F16)
        ident = sb("ident", [P, P], F32)
        ident16 = sb("ident16", [P, P], F16)
        mask = sb("mask", [P, SEQ], F32)
        bq_sb, bk_sb, bv_sb, bo_sb, b1_sb = (sb(n, [P, KB], F32) for n in ("bq_sb", "bk_sb", "bv_sb", "bo_sb", "b1_sb"))
        b0_sb = sb("b0_sb", [P, FB], F32)
        stats = sb("stats", [P, TT, 2, 6], F32)
        mv = sb("mv", [P, TT, 2], F32)
        var_eps = sb("var_eps", [P, TT], F32)
        rstd = sb("rstd", [P, TT], F32)
        minus_half = sb("minus_half", [P, TT], F32)
        row_max = sb("row_max", [P, HB], F32)
        row_sum = sb("row_sum", [P, HB], F32)
        row_inv = sb("row_inv", [P, HB], F32)

        pj = [psum(f"pj{b}") for b in range(3)]
        bank_t = [psum("bank_t0"), psum("bank_t1")]
        bank_s = psum("bank_s")
        bank_av = psum("bank_av", 2 * TOKENS)

        x_landed = [sem(f"x_landed{n}") for n in range(2 * TT)]
        ctx_landed, bias_landed = sem("ctx_landed"), sem("bias_landed")
        landed = [sem(f"landed{s}") for s in range(SLOTS)]
        hi_done = [sem(f"hi_done{s}") for s in range(SLOTS)]
        ready = [sem(f"ready{s}") for s in range(SLOTS)]
        ctx_hi_done, ctx_ready = sem("ctx_hi_done"), sem("ctx_ready")
        products = sem("products")
        pj_taken = [sem(f"pj_taken{b}") for b in range(3)]
        t_full = [sem("t_full0"), sem("t_full1")]
        t_taken = [sem("t_taken0"), sem("t_taken1")]
        ln_full = [sem("ln_full0"), sem("ln_full1")]
        ln_hi = [sem("ln_hi0"), sem("ln_hi1")]
        ln_taken = [sem("ln_taken0"), sem("ln_taken1")]
        s_full, s_taken = sem("s_full"), sem("s_taken")
        av_full, av_taken = sem("av_full"), sem("av_taken")
        v_hi_done, pd_hi_done = sem("v_hi_done"), sem("pd_hi_done")
        at_hi_done = sem("at_hi_done")
        exp_done, probs_ready = sem("exp_done"), sem("probs_ready")
        soft_step, ln_step = sem("soft_step"), sem("ln_step")
        var_done, rstd_done, xn_done = sem("var_done"), sem("rstd_done"), sem("xn_done")
        gel_done, hidden_done = sem("gel_done"), sem("hidden_done")
        e_done, res_done = sem("e_done"), sem("res_done")
        const_set, const_done = sem("const_set"), sem("const_done")
        pd_cleared = sem("pd_cleared")
        stored = sem("stored")

        START = 1

        def wait(eng, s, value):
            if not (isinstance(value, int) and value <= 0):
                eng.wait_ge(s, value)

        def pair_tiles(i):
            return [(0, 0), (1, 2)] if STAGES[i][0] == "cross" else [(0, 0), (1, 1), (2, 2)]

        def pair_source(i, p, s):
            if STAGES[i][0] == "cross":
                return (xWq, xWkv)[s][bass.ds(p, 1)]
            return (sWq, sWk, sWv)[s][bass.ds(p, 1)]

        def tile_cols(i, s, in_pairs=True):
            return 2 * CKB if in_pairs and STAGES[i][0] == "cross" and s == 1 else KB

        block = stack.enter_context(nc.Block())

        def after_pair(i, p, which):
            kind = STAGES[i][0]
            slots = {w: s for s, w in pair_tiles(i)}
            if which not in slots:
                return None
            s = slots[which]
            if isinstance(p, int) and p == PAIRS - 1:
                j = next(j for j in range(4) if o_slot(kind, j) == s)
                return o_tile(i, j)
            return s, slot_uses_before(i, s) + p + 1, pair_source(i, p + 1, s), tile_cols(i, s)

        def o_tile(i, j):
            kind = STAGES[i][0]
            return o_slot(kind, j), o_slot_use(i, j), (xWo if kind == "cross" else sWo)[j:j + 1], KB

        def early_o_tiles(i):
            return [o_tile(i, j) for j in range(2 if STAGES[i][0] == "cross" else 1)]

        def first_tile(i, s):
            if i == len(STAGES):
                return None
            if STAGES[i][0] == "ffn":
                return s, slot_uses_before(i, s), fW[s:s + 1], KB
            if s in [t[0] for t in pair_tiles(i)]:
                return s, slot_uses_before(i, s), pair_source(i, 0, s), tile_cols(i, s)
            return None

        def after_o(i, j):
            if j < 4:
                return o_tile(i, j + 4)
            return first_tile(i + 1, o_slot(STAGES[i][0], j))

        def after_ffn(i, j):
            if isinstance(j, int) and j >= FFN_TILES - 4:
                return first_tile(i + 1, j % 4)
            s = j[1] if isinstance(j, tuple) else j % 4
            at = j[0] if isinstance(j, tuple) else j
            use = slot_uses_before(i, s) + (j[2] if isinstance(j, tuple) else j // 4) + 1
            return s, use, fW[bass.ds(at + 4, 1)], KB

        @block.sync
        def _(sp):
            def load(tile):
                if tile is None:
                    return
                s, use, src, blocks = tile
                sp.wait_ge(ready[s], use + START)
                sp.dma_start(raw[:, s, 0:blocks, :], src.rearrange("a p k f -> (a p) k f")).then_inc(landed[s], 16)

            def load_x(n):
                sp.dma_start(res[:, n // TT, n % TT, :], x[n]).then_inc(x_landed[n], 16)

            for n in range(TT):
                load_x(n)
            load(first_tile(0, 0))
            sp.dma_start(ctx_raw[:], ctxT[0]).then_inc(ctx_landed, 16)
            load(first_tile(0, 1))
            for n in range(TT, 2 * TT):
                load_x(n)
            for i in range(ATTN_STAGES):
                for p in [0]:
                    for w in range(3):
                        load(after_pair(i, 0, w))
                    for tile in early_o_tiles(i):
                        load(tile)
                with sp.Fori(1, PAIRS - 1) as p:
                    for w in range(3):
                        load(after_pair(i, p, w))
                for w in range(3):
                    load(after_pair(i, PAIRS - 1, w))
                for j in range(KB):
                    if i == 0 and j == 0:
                        sp.wait_ge(ctx_ready, 1)
                        sp.dma_start(ctx_raw[:], ctxT[1]).then_inc(ctx_landed, 16)
                    load(after_o(i, j))
            for i in range(ATTN_STAGES, len(STAGES)):
                half = STAGES[i][1]

                def store(o, i=i, half=half):
                    sp.wait_ge(res_done, o + ((i - ATTN_STAGES) * KB + 1))
                    cols = bass.ds(o * P, P)
                    sp.dma_start(out[half, :, :, cols].rearrange("t p f -> p t f"), res[:, half, :, cols]).then_inc(stored, 16)

                for s in range(SLOTS):
                    load(after_ffn(i, s))
                if i > ATTN_STAGES:
                    store_last()
                with sp.Fori(1, FB // 4) as g:
                    for s in range(SLOTS):
                        load(after_ffn(i, (g * 4 + s, s, g)))
                for s in range(SLOTS):
                    load(after_ffn(i, FB + s))
                with sp.Fori(1, KB - 1) as o:
                    for s in range(SLOTS):
                        load(after_ffn(i, (FB + o * 4 + s, s, FB // 4 + o)))
                    store(o - 1)
                for s in range(SLOTS):
                    load(after_ffn(i, FFN_TILES - 4 + s))

                def store_last(store=store):
                    for o in range(KB - 2, KB):
                        store(o)
            store_last()
            sp.wait_ge(stored, 16 * 2 * KB)

        @block.scalar
        def _(act):
            for n, (dst, src) in enumerate([(bq_sb, bq), (bk_sb, bk), (bv_sb, bv), (bo_sb, bo), (b1_sb, b1), (b0_sb, b0)]):
                act.dma_start(dst[:], src).then_inc(bias_landed, 16)

            def round_tile(tile, freed):
                if tile is None:
                    return
                s, use, _, blocks = tile
                act.wait_ge(landed[s], 16 * (use + 1))
                wait(act, products, freed)
                nc.scalar.activation(w_hi[:, s, 0:blocks, :], raw[:, s, 0:blocks, :], ACT.Copy).then_inc(hi_done[s], 1)

            def round_ctx(n):
                act.wait_ge(ctx_landed, 16 * (n + 1))
                nc.scalar.activation(ctx_hi[:], ctx_raw[:], ACT.Copy).then_inc(ctx_hi_done, 1)

            def evacuate(dst, src, bias):
                if bias is None:
                    return nc.scalar.activation(dst, src, ACT.Copy)
                return nc.scalar.activation(dst, src, ACT.Identity, bias=bias)

            def take_pair(i, p, *between):
                self_attn = STAGES[i][0] == "self"
                col = bass.ds(p, 1)
                act.wait_ge(products, pair_product(i, p, 0) + 1)
                round_tile(after_pair(i, p, 0), pair_product(i, p, 0) + 1)
                for step in between:
                    step()
                wait(act, s_full, PAIRS * i + p)
                evacuate(qT[:], pj[0][:], bq_sb[:, col] if self_attn else None).then_inc(pj_taken[0], 1)
                act.wait_ge(products, pair_product(i, p, 1) + 1)
                evacuate(kT[:], pj[1][:], bk_sb[:, col] if self_attn else None).then_inc(pj_taken[1], 1)
                round_tile(after_pair(i, p, 1), pair_product(i, p, 1) + 1)
                act.wait_ge(products, pair_product(i, p, 2) + 1)
                if not isinstance(p, int) or p > 0:
                    act.wait_ge(t_full[0], pair_t_uses(i, p))
                evacuate(vT[:], pj[2][:], bv_sb[:, col] if self_attn else None).then_inc(pj_taken[2], 1)
                round_tile(after_pair(i, p, 2), pair_product(i, p, 2) + 1)

            def exp_pair(i, p):
                scale = HEAD_DIM ** -0.5 if STAGES[i][0] == "cross" else 1.0 / 4.0
                act.wait_ge(s_taken, PAIRS * i + p + 1 + START)
                nc.scalar.activation(probs[:], probs[:], ACT.Exp, scale=scale).then_inc(exp_done, 1)

            def values_hi(i, p):
                wait(act, av_full, PAIRS * i + p)
                act.wait_ge(t_full[0], pair_t_uses(i, p) + 1)
                nc.scalar.activation(v_hi[:].rearrange("p t d -> p (t d)"), bank_t[0][:], ACT.Copy).then_inc(v_hi_done, 1)

            def probs_hi(i, p):
                act.wait_ge(t_full[1], pair_t_uses(i, p) + 1)
                for b in range(2):
                    rows = slice(SEQ * b, SEQ * (b + 1))
                    nc.scalar.activation(pd_hi[rows, :, :, b, :], bank_t[1][rows].rearrange("p (t h q) -> p t h q", t=TT, h=2),
                                         ACT.Copy).then_inc(pd_hi_done, 1)

            def attn_hi(i, p):
                act.wait_ge(av_full, PAIRS * i + p + 1)
                for h in range(2):
                    head = slice(HEAD_DIM * h, HEAD_DIM * (h + 1))
                    nc.scalar.activation(at_hi[head, bass.ds(p, 1), :].rearrange("p a (t q) -> p (a t) q", t=TT),
                                         bank_av[head].rearrange("p (t h q) -> p t h q", t=TT, h=2)[:, :, h, :],
                                         ACT.Copy).then_inc(at_hi_done, 1)

            def normalised(n, t):
                kind, half = STAGES[n]
                ffn = kind == "ffn"
                for g in range(2):
                    act.wait_ge(ln_full[g], ln_tiles(n, t) + 1)
                    dst = xn_hi[:, half, 4 * g:4 * g + 4, bass.ds(t * P, P)]
                    src = bank_t[g][:, 0:256].bitcast(F16) if ffn else bank_t[g][:]
                    nc.scalar.activation(dst, src.rearrange("p (k t) -> p k t", k=4), ACT.Copy)\
                        .then_inc(ln_taken[g] if ffn else ln_hi[g], 1)

            normalised(0, 0)
            round_tile(first_tile(0, 0), 0)
            normalised(0, 1)
            round_ctx(0)
            normalised(0, 2)
            normalised(0, 3)
            round_tile(first_tile(0, 1), 0)
            for i in range(ATTN_STAGES):
                if STAGES[i][0] == "self":
                    act.wait_ge(bias_landed, 16 * 6)
                take_pair(i, 0)
                for tile in early_o_tiles(i):
                    round_tile(tile, products_before(i))

                def pair_step(p, out_before=True, norm=False):
                    if norm:
                        normalised(i + 1, p - 2)
                    if out_before:
                        attn_hi(i, p - 2)
                    values_hi(i, p - 1)
                    exp_pair(i, p - 1)
                    take_pair(i, p, lambda: probs_hi(i, p - 1))

                pair_step(1, out_before=False)
                with act.Fori(2, 2 + TT) as p:
                    pair_step(p, norm=True)
                for p in range(2 + TT, PAIRS):
                    pair_step(p)
                attn_hi(i, PAIRS - 2)
                values_hi(i, PAIRS - 1)
                exp_pair(i, PAIRS - 1)
                probs_hi(i, PAIRS - 1)
                attn_hi(i, PAIRS - 1)
                for j in range(KB):
                    b = O_BANKS[j]
                    act.wait_ge(products, o_product(i, j) + 1)
                    act.wait_ge(t_full[j % 2], o_t_uses(i, j))
                    evacuate(o_T[j % 2][:], pj[b][:], bo_sb[:, j:j + 1] if STAGES[i][0] == "self" else None).then_inc(pj_taken[b], 1)
                    if i == 0 and j == KB // 2:
                        round_ctx(1)
                    round_tile(after_o(i, j), o_product(i, j) + 1)
            for i in range(ATTN_STAGES, len(STAGES)):
                before = products_before(i)
                gelus = (i - ATTN_STAGES) * FB

                def gelu(j, s):
                    act.wait_ge(products, before + j + 1)
                    wait(act, hidden_done, gelus + j - 1)
                    nc.scalar.activation(gel[:, s % 2, :], pj[s % 2][:], ACT.Gelu, bias=b0_sb[:, bass.ds(j, 1)]).then_inc(gel_done, 1)

                def first_group():
                    for s in range(SLOTS):
                        gelu(s, s)
                        round_tile(after_ffn(i, s), before + s + 1)

                first_group()
                if i == ATTN_STAGES:
                    for s in range(SLOTS):
                        gelu(SLOTS + s, s)
                        normalised(i + 1, s)
                        round_tile(after_ffn(i, SLOTS + s), before + SLOTS + s + 1)
                with act.Fori(2 if i == ATTN_STAGES else 1, FB // 4) as g:
                    for s in range(SLOTS):
                        gelu(g * 4 + s, s)
                        round_tile(after_ffn(i, (g * 4 + s, s, g)), g * 4 + (before + s + 1))

                def take_out(o, b, tiles):
                    for s in range(SLOTS):
                        act.wait_ge(products, o * 4 + (before + FB + s + 1))
                        if s == SLOTS - 1:
                            act.wait_ge(t_full[b], ffn_t_uses(i, 0) + o_half(o, b))
                            nc.scalar.activation(e_T[:, b, :], pj[b][:], ACT.Identity, bias=b1_sb[:, bass.ds(o, 1)]).then_inc(e_done, 1)
                        round_tile(tiles[s], o * 4 + (before + FB + s + 1))

                with act.Fori(0, KB // 2 - 1) as g:
                    for b in range(2):
                        def o_half(o, b, g=g):
                            return g
                        take_out(g * 2 + b, b, [after_ffn(i, (g * 8 + (FB + 4 * b + s), s, g * 2 + (FB // 4 + b))) for s in range(SLOTS)])
                for o in range(KB - 2, KB):
                    def o_half(o, b):
                        return o // 2
                    take_out(o, o % 2, [after_ffn(i, FB + 4 * o + s) for s in range(SLOTS)])

        def lower(engine, eng, tile):
            if tile is None:
                return
            s, use, _, blocks = tile
            eng.wait_ge(hi_done[s], use + 1)
            engine.tensor_tensor(w_lo[:, s, 0:blocks, :], raw[:, s, 0:blocks, :], w_hi[:, s, 0:blocks, :].bitcast(F32),
                                 ALU.subtract).then_inc(ready[s], 1)

        @block.gpsimd
        def _(pool):
            nc.gpsimd.memset(minus_half[:], -0.5).then_inc(const_set, 1)
            nc.gpsimd.memset(ident[:], 0.0).then_inc(const_set, 1)
            nc.gpsimd.memset(mask[:], 0.0).then_inc(const_set, 1)
            pool.wait_ge(const_set, 3)
            nc.gpsimd.affine_select(out=ident[:], in_=ident[:], compare_op=ALU.not_equal, fill=1.0, base=0,
                                    pattern=[[-1, P]], channel_multiplier=1).then_inc(const_set, 1)
            pool.wait_ge(const_set, 4)
            nc.gpsimd.tensor_copy(ident16[:], ident[:]).then_inc(const_done, 1)

            def lower_ctx(n):
                pool.wait_ge(ctx_hi_done, n + 1)
                nc.gpsimd.tensor_tensor(ctx_lo[:], ctx_raw[:], ctx_hi[:].bitcast(F32), ALU.subtract).then_inc(ctx_ready, 1)

            def inverse_root(n):
                pool.wait_ge(var_done, TT + n)
                nc.gpsimd.tensor_tensor(rstd[:], var_eps[:], minus_half[:], ALU.pow).then_inc(rstd_done, 1)

            for t in range(TT):
                pool.wait_ge(var_done, t + 1)
                nc.gpsimd.tensor_tensor(rstd[:, t:t + 1], var_eps[:, t:t + 1], minus_half[:, t:t + 1], ALU.pow).then_inc(rstd_done, 1)
            lower(nc.gpsimd, pool, first_tile(0, 0))
            lower_ctx(0)
            lower(nc.gpsimd, pool, first_tile(0, 1))
            pool.wait_ge(ready[1], 1 + START)
            for h in range(2):
                part = slice(SEQ * h, SEQ * (h + 1))
                pool.wait_ge(const_done, 1 + h)
                nc.gpsimd.affine_select(out=mask[part], in_=mask[part], compare_op=ALU.is_ge, fill=MASKED, base=0,
                                        pattern=[[-1, SEQ]], channel_multiplier=1).then_inc(const_done, 1)
            pool.wait_ge(const_done, 3)
            nc.gpsimd.memset(pd_hi[:].bitcast(F32), 0.0).then_inc(pd_cleared, 1)
            nc.gpsimd.memset(pd_lo[:].bitcast(F32), 0.0).then_inc(pd_cleared, 1)
            for i in range(ATTN_STAGES):
                pool_tiles = range(1, 3) if STAGES[i][0] == "cross" else range(3)
                if 0 in pool_tiles:
                    lower(nc.gpsimd, pool, after_pair(i, 0, 0))
                inverse_root(i + 1)
                for w in range(1, 3):
                    lower(nc.gpsimd, pool, after_pair(i, 0, w))
                for tile in early_o_tiles(i):
                    lower(nc.gpsimd, pool, tile)
                with pool.Fori(1, PAIRS - 1) as p:
                    for w in pool_tiles:
                        lower(nc.gpsimd, pool, after_pair(i, p, w))
                for w in pool_tiles:
                    lower(nc.gpsimd, pool, after_pair(i, PAIRS - 1, w))
                for j in range(KB):
                    if i == 0 and j == KB // 2:
                        lower_ctx(1)
                    lower(nc.gpsimd, pool, after_o(i, j))
            lower(nc.gpsimd, pool, after_ffn(ATTN_STAGES, 0))
            inverse_root(ATTN_STAGES + 1)
            for s in range(1, SLOTS):
                lower(nc.gpsimd, pool, after_ffn(ATTN_STAGES, s))

        @block.vector
        def _(dve):
            ln_steps = 0

            def ordered(instruction):
                nonlocal ln_steps
                instruction.then_inc(ln_step, 1)
                ln_steps += 1
                dve.wait_ge(ln_step, ln_steps)

            def statistics(n, tiles):
                half = STAGES[n][1]
                for t in tiles:
                    if n < 2:
                        dve.wait_ge(x_landed[half * TT + t], 16)
                    for g in range(2):
                        last = nc.vector.bn_stats(stats[:, t, g, :], res[:, half, t, g * 512:(g + 1) * 512])
                ordered(last)
                for t in tiles:
                    last = nc.vector.bn_aggr(mv[:, t, :], stats[:, t, :, :].rearrange("p g s -> p (g s)"))
                ordered(last)
                cols = slice(tiles[0], tiles[-1] + 1)
                nc.vector.tensor_scalar(var_eps[:, cols], mv[:, cols, 1], LN_EPS, None, ALU.add).then_inc(var_done, 1)

            def scale_tile(n, t, buffer):
                dve.wait_ge(rstd_done, t + 1 if n == 0 else TT + n)
                here = bass.ds(t, 1)
                nc.vector.tensor_scalar(buffer, res[:, STAGES[n][1], here, :].rearrange("p a f -> p (a f)"),
                                        mv[:, here, 0], rstd[:, here], ALU.subtract, ALU.mult).then_inc(xn_done, 1)

            def norm_lo(n, t):
                kind, half = STAGES[n]
                if kind == "ffn":
                    return
                for g in range(2):
                    dve.wait_ge(ln_hi[g], ln_tiles(n, t) + 1)
                    cols = (slice(None), slice(4 * g, 4 * g + 4), bass.ds(t * P, P))
                    nc.vector.tensor_tensor(xn_lo[half][cols], bank_t[g][:].rearrange("p (k t) -> p k t", k=4),
                                            xn_hi[:, half][cols].bitcast(F32), ALU.subtract).then_inc(ln_taken[g], 1)

            def by_batch(ap):
                return ap.unsqueeze(2).to_broadcast([P, HB, SEQ])

            def softmax(i, p, *between):
                self_attn = STAGES[i][0] == "self"
                n = PAIRS * i + p
                t_uses = pair_t_uses(i, p)
                scores = bank_s[:].rearrange("p (b k) -> p b k", b=HB)
                dve.wait_ge(s_full, n + 1)
                dve.wait_ge(t_full[1], t_uses)
                if not self_attn:
                    if isinstance(n, int) and n == 0:
                        dve.wait_ge(const_done, 3)
                    nc.vector.tensor_tensor(probs[:], scores, mask[:].unsqueeze(1).to_broadcast([P, HB, SEQ]),
                                            ALU.add).then_inc(soft_step, 1)
                    dve.wait_ge(soft_step, soft_steps(i, p, 1))
                    scores = probs[:]
                k = 0 if self_attn else 1
                nc.vector.tensor_reduce(row_max[:], scores, AX.X, ALU.max).then_inc(soft_step, 1)
                dve.wait_ge(soft_step, soft_steps(i, p, k + 1))
                nc.vector.tensor_tensor(probs[:], scores, by_batch(row_max[:]), ALU.subtract).then_inc(s_taken, 1)
                for step in between:
                    step()
                dve.wait_ge(exp_done, n + 1)
                nc.vector.tensor_reduce(row_sum[:], probs[:], AX.X, ALU.add).then_inc(soft_step, 1)
                dve.wait_ge(soft_step, soft_steps(i, p, k + 2))
                nc.vector.reciprocal(row_inv[:], row_sum[:]).then_inc(soft_step, 1)
                dve.wait_ge(soft_step, soft_steps(i, p, k + 3))
                nc.vector.tensor_tensor(probs[:], probs[:], by_batch(row_inv[:]), ALU.mult).then_inc(probs_ready, 1)

            def values_lo(i, p):
                dve.wait_ge(v_hi_done, PAIRS * i + p + 1)
                nc.vector.tensor_tensor(v_lo[:].rearrange("p t d -> p (t d)"), bank_t[0][:],
                                        v_hi[:].rearrange("p t d -> p (t d)").bitcast(F32), ALU.subtract).then_inc(t_taken[0], 1)

            def probs_lo(i, p):
                for b in range(2):
                    rows = slice(SEQ * b, SEQ * (b + 1))
                    dve.wait_ge(pd_hi_done, (PAIRS * i + p) * 2 + (b + 1))
                    last = nc.vector.tensor_tensor(pd_lo[rows, :, :, b, :],
                                                   bank_t[1][rows].rearrange("p (t h q) -> p t h q", t=TT, h=2),
                                                   pd_hi[rows, :, :, b, :].bitcast(F32), ALU.subtract)
                last.then_inc(t_taken[1], 1)

            def attn_lo(i, p):
                at = bass.ds(p, 1)
                for h in range(2):
                    head = slice(HEAD_DIM * h, HEAD_DIM * (h + 1))
                    dve.wait_ge(at_hi_done, (PAIRS * i + p) * 2 + (h + 1))
                    last = nc.vector.tensor_tensor(at_lo[head, at, :].rearrange("p a (t q) -> p (a t) q", t=TT),
                                                   bank_av[head].rearrange("p (t h q) -> p t h q", t=TT, h=2)[:, :, h, :],
                                                   at_hi[head, at, :].rearrange("p a (t q) -> p (a t) q", t=TT).bitcast(F32),
                                                   ALU.subtract)
                last.then_inc(av_taken, 1)

            def soft_steps(i, p, k):
                per = {"cross": 4, "self": 3}
                before = sum(per[STAGES[n][0]] * PAIRS for n in range(i))
                return p * per[STAGES[i][0]] + (before + k)

            statistics(0, [0])
            statistics(0, [1])
            scale_tile(0, 0, xn[:, 0, :])
            statistics(0, [2])
            scale_tile(0, 1, xn[:, 1, :])
            norm_lo(0, 0)
            statistics(0, [3])
            for t in range(2, TT):
                dve.wait_ge(ln_full[1], t - 1)
                scale_tile(0, t, xn[:, t % 2, :])
                norm_lo(0, t - 1)
            norm_lo(0, TT - 1)
            for i in range(ATTN_STAGES):
                half = STAGES[i][1]
                statistics(i + 1, range(TT))
                one_tile = xn[:, 0, 0:HIDDEN // 2].bitcast(F16) if STAGES[i + 1][0] == "ffn" else xn[:, 0, :]

                cross = STAGES[i][0] == "cross"
                if cross:
                    lower(nc.vector, dve, after_pair(i, 0, 0))

                def attend(p, scale_next=False, norm=False):
                    if norm:
                        norm_lo(i + 1, p - 1)
                    softmax(i, p, lambda: values_lo(i, p))
                    if not isinstance(p, int) or p > 0:
                        attn_lo(i, p - 1)
                    if scale_next:
                        scale_tile(i + 1, p, one_tile)
                    if cross and not (isinstance(p, int) and p == PAIRS - 1):
                        lower(nc.vector, dve, after_pair(i, p + 1, 0))
                    probs_lo(i, p)

                attend(0, scale_next=True)
                with dve.Fori(1, TT) as p:
                    attend(p, scale_next=True, norm=True)
                attend(TT, norm=True)
                for p in range(TT + 1, PAIRS):
                    attend(p)
                attn_lo(i, PAIRS - 1)
                for j in range(KB):
                    g = j % 2
                    dve.wait_ge(t_full[g], o_t_uses(i, j) + 1)
                    here = res[:, half, :, j * P:(j + 1) * P]
                    nc.vector.tensor_tensor(here, here, bank_t[g][:].rearrange("p (t f) -> p t f", t=TT),
                                            ALU.add).then_inc(t_taken[g], 1)
                for g in range(2):
                    dve.wait_ge(t_taken[g], o_t_uses(i, KB - 1) + 1)
            for i in range(ATTN_STAGES, len(STAGES)):
                half = STAGES[i][1]
                gelus = (i - ATTN_STAGES) * FB

                def copy_hidden(j, s):
                    dve.wait_ge(gel_done, gelus + j + 1)
                    nc.vector.tensor_copy(hidden[:, bass.ds(j, 1), :].rearrange("p a t -> p (a t)"), gel[:, s % 2, :]).then_inc(hidden_done, 1)

                if i == ATTN_STAGES:
                    statistics(i + 1, range(TT))
                for s in range(SLOTS):
                    copy_hidden(s, s)
                    if i == ATTN_STAGES and s == 1:
                        for t in range(TT):
                            scale_tile(i + 1, t, ffn_tiles[:, t, :])
                    if i > ATTN_STAGES:
                        lower(nc.vector, dve, after_ffn(i, s))
                with dve.Fori(1, FB // 4) as g:
                    for s in range(SLOTS):
                        copy_hidden(g * 4 + s, s)
                        lower(nc.vector, dve, after_ffn(i, (g * 4 + s, s, g)))

                def add_out(o, b, half_o):
                    dve.wait_ge(t_full[b], half_o + (ffn_t_uses(i, 0) + 1))
                    here = res[:, half, :, bass.ds(o * P, P)]
                    nc.vector.tensor_tensor(here, here, bank_t[b][:, 0:256].bitcast(F16).rearrange("p (t f) -> p t f", t=TT),
                                            ALU.add).then_inc(res_done, 1)

                def out_step(o, tiles, add):
                    for s in range(SLOTS):
                        lower(nc.vector, dve, tiles[s])
                        if s == 1 and add:
                            add_out(*add)

                def later_tiles(g, b):
                    return [after_ffn(i, (g * 8 + (FB + 4 * b + s), s, g * 2 + (FB // 4 + b))) for s in range(SLOTS)]

                out_step(0, [after_ffn(i, FB + s) for s in range(SLOTS)], None)
                out_step(1, [after_ffn(i, FB + 4 + s) for s in range(SLOTS)], (0, 0, 0))
                with dve.Fori(1, KB // 2 - 1) as g:
                    out_step(g * 2, later_tiles(g, 0), (g * 2 - 1, 1, g - 1))
                    out_step(g * 2 + 1, later_tiles(g, 1), (g * 2, 0, g))
                for o in range(KB - 2, KB):
                    out_step(o, [after_ffn(i, FB + 4 * o + s) for s in range(SLOTS)], (o - 1, (o - 1) % 2, (o - 1) // 2))
                add_out(KB - 1, 1, KB // 2 - 1)

        @block.tensor
        def _(pe):
            for s in [*ready, *pj_taken, s_taken, av_taken]:
                pe.sem_inc(s, START)
            pe.wait_ge(const_done, 1)

            def accumulate(bank, terms, start=True, stop=True):
                for n, (lhs, rhs) in enumerate(terms):
                    last = nc.tensor.matmul(bank[:], lhs, rhs, start=start and n == 0, stop=stop and n == len(terms) - 1)
                return last

            def exact(s, blocks, hi, lo):
                for n, k in enumerate(blocks):
                    yield w_hi[:, s, k, :], hi[:, n, :]
                    yield w_hi[:, s, k, :], lo[:, n, :]
                    yield w_lo[:, s, k, :], hi[:, n, :]

            def tile_ready(s, use):
                pe.wait_ge(ready[s], use + 1 + START)

            def project(i, p, which, *between):
                kind, half = STAGES[i]
                pe.wait_ge(pj_taken[which], bank_uses_before(i, which) + p + START)
                s = which if kind == "self" else min(which, 1)
                if which == 0 or kind == "self" or which == 1:
                    tile_ready(s, slot_uses_before(i, s) + p)
                if kind == "cross" and which:
                    blocks, hi, lo = range(CKB * (which - 1), CKB * which), ctx_hi, ctx_lo
                else:
                    blocks, hi, lo = range(KB), xn_hi[:, half], xn_lo[half]
                cuts = [0, *(block for block, _ in between), len(blocks)]
                for n, (first, end) in enumerate(zip(cuts, cuts[1:])):
                    if n:
                        between[n - 1][1]()
                    if first < end:
                        terms = list(exact(s, blocks[first:end], hi[:, first:end], lo[:, first:end]))
                        last = accumulate(pj[which], terms, start=first == 0, stop=end == len(blocks))
                last.then_inc(products, 1)

            def scores_inputs(i, p):
                n = PAIRS * i + p
                pe.wait_ge(pj_taken[0], bank_uses_before(i, 0) + p + 1 + START)
                pe.wait_ge(pj_taken[1], bank_uses_before(i, 1) + p + 1 + START)
                pe.wait_ge(s_taken, n + START)

            def scores():
                for b in range(HB):
                    cols = slice(SEQ * b, SEQ * (b + 1))
                    for h in range(2):
                        head = slice(HEAD_DIM * h, HEAD_DIM * (h + 1))
                        last = nc.tensor.matmul(bank_s[head, cols], qT[head, cols], kT[head, cols], start=True, stop=True)
                last.then_inc(s_full, 1)

            def transpose_v(i, p, normed=False):
                if normed:
                    for g in range(2):
                        pe.wait_ge(ln_taken[g], ln_tiles(i + 1, p))
                pe.wait_ge(pj_taken[2], bank_uses_before(i, 2) + p + 1 + START)
                pe.wait_ge(t_taken[0], pair_t_uses(i, p))
                for t in range(TT):
                    cols = slice(t * P, (t + 1) * P)
                    last = nc.tensor.transpose(bank_t[0][:, cols], vT[:, cols], ident[:])
                last.then_inc(t_full[0], 1)

            def transpose_probs(i, p):
                pe.wait_ge(probs_ready, PAIRS * i + p + 1)
                pe.wait_ge(t_taken[1], pair_t_uses(i, p))
                flat = probs[:].rearrange("p b k -> p (b k)")
                for t in range(TT):
                    cols = slice(t * P, (t + 1) * P)
                    last = nc.tensor.transpose(bank_t[1][:, cols], flat[:, cols], ident[:])
                last.then_inc(t_full[1], 1)

            def weigh_values(i, p):
                if isinstance(i, int) and i == 0 and isinstance(p, int):
                    pe.wait_ge(pd_cleared, 2)
                pe.wait_ge(t_taken[0], pair_t_uses(i, p) + 1)
                pe.wait_ge(t_taken[1], pair_t_uses(i, p) + 1)
                pe.wait_ge(av_taken, PAIRS * i + p + START)
                for t in range(TT):
                    terms = [(v[:, t, :], pd[:, t].rearrange("p h b q -> p (h b q)"))
                             for v, pd in ((v_hi, pd_hi), (v_hi, pd_lo), (v_lo, pd_hi))]
                    last = accumulate(bank_av[:, t * 2 * P:(t + 1) * 2 * P], terms)
                last.then_inc(av_full, 1)

            def normalised(n, t, tile, banks=(0, 1)):
                ffn = STAGES[n][0] == "ffn"
                pe.wait_ge(xn_done, ln_tiles(n, t) + 1)
                for g in banks:
                    for k in range(4):
                        cols = slice((4 * g + k) * P, (4 * g + k + 1) * P)
                        dst = bank_t[g][:, 0:256].bitcast(F16) if ffn else bank_t[g]
                        if k == 0:
                            wait(pe, ln_taken[g], ln_tiles(n, t))
                            if 0 < n <= ATTN_STAGES:
                                pe.wait_ge(t_taken[g], pair_t_uses(n - 1, t) + 1)
                            elif n:
                                pe.wait_ge(t_taken[g], ffn_t_uses(ATTN_STAGES, 0))
                        last = nc.tensor.transpose(dst[:, k * P:(k + 1) * P], tile[:, cols], (ident16 if ffn else ident)[:])
                    last.then_inc(ln_full[g], 1)

            def xn_is_ready(i, g):
                pe.wait_ge(ln_taken[g], ln_tiles(i + 1, 0))

            for t in range(TT):
                normalised(0, t, xn[:, t % 2, :])
            finish = None
            for i in range(ATTN_STAGES):
                kind, half = STAGES[i]
                xn_is_ready(i, 0)
                project(i, 0, 0, *([(2, finish)] if finish else []), (KB // 2, lambda: xn_is_ready(i, 1)))
                if kind == "cross":
                    pe.wait_ge(ctx_ready, i + 1)
                project(i, 0, 1)
                project(i, 0, 2)
                one_tile = xn[:, 0, 0:HIDDEN // 2].bitcast(F16) if STAGES[i + 1][0] == "ffn" else xn[:, 0, :]
                probs_at = CKB // 2 if kind == "cross" else KB // 2

                def pair_step(p, values_before=True, norm=False):
                    if norm:
                        normalised(i + 1, p - 2, one_tile, banks=[0])

                    def attend_inputs():
                        scores_inputs(i, p - 1)
                        if norm:
                            normalised(i + 1, p - 2, one_tile, banks=[1])

                    def attend():
                        scores()
                        if values_before:
                            weigh_values(i, p - 2)

                    project(i, p, 0, (1, attend_inputs), (2, attend), (3, lambda: transpose_v(i, p - 1, norm)))
                    project(i, p, 1, (probs_at, lambda: transpose_probs(i, p - 1)))
                    project(i, p, 2)

                pair_step(1, values_before=False)
                with pe.Fori(2, 2 + TT) as p:
                    pair_step(p, norm=True)
                with pe.Fori(2 + TT, PAIRS) as p:
                    pair_step(p)

                last = PAIRS - 1

                def o_part(j, blocks, start, stop):
                    s, b = o_slot(kind, j), O_BANKS[j]
                    if start:
                        pe.wait_ge(pj_taken[b], bank_uses_before(i, b) + PAIRS + j // 3 + START)
                        tile_ready(s, o_slot_use(i, j))
                    terms = list(exact(s, blocks, at_hi[:, blocks.start:blocks.stop], at_lo[:, blocks.start:blocks.stop]))
                    return accumulate(pj[b], terms, start, stop)

                def open_tiles(*parts):
                    for j, first, end in parts:
                        o_part(j, range(first, end), first == 0, False)

                opened = (KB - 1, KB - 3, KB // 2)
                pe.wait_ge(av_taken, PAIRS * i + last - 1 + START)
                open_tiles((0, 0, 1))
                scores_inputs(i, last)
                open_tiles((0, 1, 2))
                scores()
                weigh_values(i, last - 1)
                transpose_v(i, last)
                open_tiles((0, 2, 6), (1, 0, 2))
                transpose_probs(i, last)
                open_tiles((1, 2, opened[1]))
                pe.wait_ge(av_taken, PAIRS * i + last + START)
                open_tiles((0, 6, opened[0]))
                weigh_values(i, last)
                open_tiles((2, 0, opened[2]))
                pe.wait_ge(av_taken, PAIRS * i + last + 1 + START)

                def transpose_o(j, i=i):
                    g, b = j % 2, O_BANKS[j]
                    pe.wait_ge(pj_taken[b], bank_uses_before(i, b) + PAIRS + j // 3 + 1 + START)
                    pe.wait_ge(t_taken[g], o_t_uses(i, j))
                    for t in range(TT):
                        cols = slice(t * P, (t + 1) * P)
                        done = nc.tensor.transpose(bank_t[g][:, cols], o_T[g][:, cols], ident[:])
                    done.then_inc(t_full[g], 1)

                for j in range(KB):
                    if j < 3:
                        o_part(j, range(opened[j], KB), False, True).then_inc(products, 1)
                    else:
                        o_part(j, range(0, KB), True, True).then_inc(products, 1)
                    if j:
                        transpose_o(j - 1)

                def finish(transpose_o=transpose_o):
                    transpose_o(KB - 1)

            for i in range(ATTN_STAGES, len(STAGES)):
                half = STAGES[i][1]
                n = i - ATTN_STAGES
                bank_base = bank_uses_before(i, 0)
                for g in range(2):
                    xn_is_ready(i, g)

                def ffn_up(g, after=None):
                    for s in range(SLOTS):
                        b = s % 2
                        if s >= 2:
                            pe.wait_ge(gel_done, g * 4 + (n * FB + s - 1))
                        elif isinstance(g, int) and g == 0:
                            if n == 0:
                                pe.wait_ge(pj_taken[b], bank_base + START)
                            else:
                                pe.wait_ge(e_done, n * KB - 1 + s)
                        else:
                            pe.wait_ge(gel_done, g * 4 + (n * FB + s - 1))
                        tile_ready(s, slot_uses_before(i, s) + g)
                        terms = [(w[:, s, k, :], xn_hi[:, half, k, :]) for k in range(KB) for w in (w_hi, w_lo)]
                        accumulate(pj[b], terms).then_inc(products, 1)
                        if after:
                            after(s)

                def ffn_down(o, b, before=None):
                    if isinstance(o, int) and o < 2:
                        pe.wait_ge(gel_done, n * FB + FB - 1 + o)
                    else:
                        pe.wait_ge(e_done, o + (n * KB - 1))
                    for s in range(SLOTS):
                        if isinstance(o, int) and o == 0:
                            pe.wait_ge(hidden_done, n * FB + KB * (s + 1))
                        tile_ready(s, o + (slot_uses_before(i, s) + FB // 4))
                        terms = [(w[:, s, k, :], hidden[:, s * KB + k, :]) for k in range(KB) for w in (w_hi, w_lo)]
                        accumulate(pj[b], terms, start=s == 0, stop=s == SLOTS - 1).then_inc(products, 1)
                        if s == 0 and before is not None:
                            transpose_e(before, 1 - b)

                def transpose_e(o, b, n=n, i=i):
                    pe.wait_ge(e_done, o + (n * KB + 1))
                    if isinstance(o, int) and n * KB + o < 2:
                        pe.wait_ge(ln_taken[b], ln_tiles(i + 2, 0))
                    else:
                        pe.wait_ge(res_done, o + (n * KB - 1))
                    bank16 = bank_t[b][:, 0:256].bitcast(F16)
                    for t in range(TT):
                        cols = slice(t * P, (t + 1) * P)
                        done = nc.tensor.transpose(bank16[:, cols], e_T[:, b, cols], ident16[:])
                    done.then_inc(t_full[b], 1)

                if i == ATTN_STAGES:
                    ffn_up(0, lambda s: s == 0 and finish())
                    ffn_up(1, lambda s: normalised(i + 1, s, ffn_tiles[:, s, :]))
                else:
                    ffn_up(0, lambda s: s == 0 and finish())
                with pe.Fori(2 if i == ATTN_STAGES else 1, FB // 4) as g:
                    ffn_up(g)
                ffn_down(0, 0)
                ffn_down(1, 1, 0)
                with pe.Fori(1, KB // 2) as g:
                    ffn_down(g * 2, 0, g * 2 - 1)
                    ffn_down(g * 2 + 1, 1, g * 2)

                def finish(transpose_e=transpose_e):
                    transpose_e(KB - 1, 1)
            finish()


def weight_tiles(w, out_blocks, in_blocks):
    return w.reshape(out_blocks, P, in_blocks, P).transpose(0, 3, 2, 1)


def kernel(x, ctx_512, L0_xattn_Wq, L0_xattn_Wkv_expand, L0_xattn_Wout, L0_attn_Wq, L0_attn_bq, L0_attn_Wk,
           L0_attn_bk, L0_attn_Wv, L0_attn_bv, L0_attn_Wo, L0_attn_bo, L0_ffn_W0, L0_ffn_bias0, L0_ffn_W1,
           L0_ffn_bias1):
    from concourse import bacc
    from concourse.bass_utils import run_bass_kernel_spmd

    def columns(b):
        return np.asarray(b).reshape(-1, P).T

    wkv = np.asarray(L0_xattn_Wkv_expand)
    kv = [weight_tiles(wkv[n * HIDDEN:(n + 1) * HIDDEN], PAIRS, CKB) for n in range(2)]
    ctx = np.asarray(ctx_512)[:, :SEQ, :].reshape(2, TOKENS, CKB, P).transpose(0, 3, 2, 1)
    w1 = np.asarray(L0_ffn_W1).reshape(KB, P, FKB, KB, P).transpose(0, 2, 4, 3, 1).reshape(KB * FKB, P, KB, P)
    ins = {
        "x": np.asarray(x).reshape(2 * TT, P, HIDDEN),
        "ctxT": ctx,
        "xWq": weight_tiles(np.asarray(L0_xattn_Wq), PAIRS, KB),
        "xWkv": np.concatenate(kv, axis=2),
        "xWo": weight_tiles(np.asarray(L0_xattn_Wout), KB, KB),
        "sWq": weight_tiles(np.asarray(L0_attn_Wq).T, PAIRS, KB),
        "sWk": weight_tiles(np.asarray(L0_attn_Wk).T, PAIRS, KB),
        "sWv": weight_tiles(np.asarray(L0_attn_Wv).T, PAIRS, KB),
        "sWo": weight_tiles(np.asarray(L0_attn_Wo).T, KB, KB),
        "fW": np.concatenate([weight_tiles(np.asarray(L0_ffn_W0), FB, KB), w1], axis=0),
        "bq": columns(L0_attn_bq), "bk": columns(L0_attn_bk), "bv": columns(L0_attn_bv),
        "bo": columns(L0_attn_bo), "b0": columns(L0_ffn_bias0), "b1": columns(L0_ffn_bias1),
    }
    ins = {f"in_{n}": np.ascontiguousarray(a) for n, a in ins.items()}
    nc = bacc.Bacc("TRN2", target_bir_lowering=False, num_devices=1, dynamic_dma_scratch_size=1024)
    args = [nc.dram_tensor(n, a.shape, F32, kind="ExternalInput").ap() for n, a in ins.items()]
    out = nc.dram_tensor("out", (2, TT, P, HIDDEN), F32, kind="ExternalOutput").ap()
    build(nc, *args, out)
    result = run_bass_kernel_spmd(nc, [ins], core_ids=[0])
    return result.results[0]["out"].reshape(BATCHES, SEQ, HIDDEN)
```

```python
from contextlib import ExitStack

import numpy as np

import concourse.bass as bass
from concourse import mybir

F32 = mybir.dt.float32
F32R = mybir.dt.float32r
F16 = mybir.dt.float16
ALU = mybir.AluOpType
ACT = mybir.ActivationFunctionType
AX = mybir.AxisListType

P = 128
BATCHES, SEQ, HIDDEN = 16, 64, 1024
CTX = 256
FFN = 4096
HEAD_DIM = 64
LN_EPS = 1e-5
MASKED = -3.0e38

KB = HIDDEN // P
CKB = CTX // P
PAIRS = HIDDEN // (2 * HEAD_DIM)
TOKENS = BATCHES * SEQ // 2
TT = TOKENS // P
HB = BATCHES // 2
FB = FFN // P
FKB = FB // KB
SLOTS = 4

STAGES = [("cross", 0), ("cross", 1), ("self", 0), ("self", 1), ("ffn", 0), ("ffn", 1)]
ATTN_STAGES = 4

O_BANKS = [j % 3 for j in range(KB)]
O_PER_BANK = [O_BANKS.count(b) for b in range(3)]
PRODUCTS = 3 * PAIRS + KB
T_USES = PAIRS + KB // 2
FFN_TILES = FB + KB * FKB
FFN_GROUPS = FFN_TILES // SLOTS
UP_GROUPS = FB // SLOTS


def products_before(i):
    return PRODUCTS * min(i, ATTN_STAGES) + FFN_TILES * max(i - ATTN_STAGES, 0)


def first_reversed(i, p):
    return STAGES[i][0] == "cross" and isinstance(p, int) and p == 0


def pair_product(i, p, which):
    if first_reversed(i, p):
        which = 2 - which
    return products_before(i) + 3 * p + which


def o_product(i, j):
    return products_before(i) + 3 * PAIRS + j


def bank_uses_before(i, b):
    attn = min(i, ATTN_STAGES) * (PAIRS + O_PER_BANK[b])
    return attn + (max(i - ATTN_STAGES, 0) * (FB + KB) // 2 if b < 2 else 0)


def pair_t_uses(i, p):
    return T_USES * i + p


def o_t_uses(i, j):
    return T_USES * i + PAIRS + j // 2


def ffn_t_uses(i, o):
    return T_USES * ATTN_STAGES + (i - ATTN_STAGES) * KB // 2 + o // 2


def ln_tiles(n, t):
    return TT * n + t


def o_slot(j):
    return (3, 0, 1, 2)[j % SLOTS]


PAIR_TILES = {"cross": (PAIRS - 1, PAIRS, 1, 0), "self": (PAIRS, PAIRS, PAIRS, 0)}


def slot_uses_before(i, s):
    n = 0
    for kind, _ in STAGES[:i]:
        n += FFN_GROUPS if kind == "ffn" else PAIR_TILES[kind][s] + KB // SLOTS
    return n


def pair_slot(i, p, which):
    if STAGES[i][0] == "self":
        return which, slot_uses_before(i, which) + p
    if which:
        return 1, slot_uses_before(i, 1) + p
    if isinstance(p, int) and p < 2:
        return 2 * p, slot_uses_before(i, 2 * p)
    return 0, p + (slot_uses_before(i, 0) - 1)


def o_slot_use(i, j):
    kind, s = STAGES[i][0], o_slot(j)
    return slot_uses_before(i, s) + PAIR_TILES[kind][s] + j // SLOTS


def build(nc, x, ctxT, xWq, xWkv, xWo, sWq, sWk, sWv, sWo, fW, bq, bk, bv, bo, b0, b1, out):
    with ExitStack() as stack:
        def sb(name, shape, dt):
            return stack.enter_context(nc.sbuf_tensor(name, shape, dt))

        def psum(name, cols=TOKENS):
            return stack.enter_context(nc.psum_tensor(name, [P, cols], F32))

        def sem(name):
            return stack.enter_context(nc.semaphore(name))

        res = sb("res", [P, 2, TT, HIDDEN], F32)
        xn_hi = sb("xn_hi", [P, 2, KB, TOKENS], F32R)
        low = sb("low", [P, 4, KB, TOKENS], F32R)
        xn_lo = [low[:, 0], low[:, 3]]
        at_hi, at_lo = low[:, 1], low[:, 2]
        hidden = low[:, :].rearrange("p a k t -> p (a k) t")
        raw = sb("raw", [P, SLOTS, KB, P], F32)
        w_hi = sb("w_hi", [P, SLOTS, KB, P], F32R)
        w_lo = sb("w_lo", [P, SLOTS, KB, P], F32R)
        ctx_raw = sb("ctx_raw", [P, CKB, TOKENS], F32)
        ctx_hi = sb("ctx_hi", [P, CKB, TOKENS], F32R)
        ctx_lo = sb("ctx_lo", [P, CKB, TOKENS], F32R)
        qT = sb("qT", [P, TOKENS], F32)
        kT = sb("kT", [P, TOKENS], F32)
        vT = sb("vT", [P, TOKENS], F32)
        v_hi = sb("v_hi", [P, TT, P], F32R)
        v_lo = sb("v_lo", [P, TT, P], F32R)
        probs = sb("probs", [P, HB, SEQ], F32)
        pd_hi = sb("pd_hi", [P, TT, 2, 2, SEQ], F32R)
        pd_lo = sb("pd_lo", [P, TT, 2, 2, SEQ], F32R)
        o_T = [kT, vT]
        xn = sb("xn", [P, 2, HIDDEN], F32)
        ffn_tiles = xn[:].rearrange("p a f -> p (a f)").bitcast(F16).rearrange("p (t f) -> p t f", t=TT)
        gel = sb("gel", [P, 2, TOKENS], F16)
        e_T = sb("e_T", [P, 2, TOKENS], F16)
        ident = sb("ident", [P, P], F32)
        ident16 = sb("ident16", [P, P], F16)
        mask = sb("mask", [P, SEQ], F32)
        bq_sb, bk_sb, bv_sb, bo_sb, b1_sb = (sb(n, [P, KB], F32) for n in ("bq_sb", "bk_sb", "bv_sb", "bo_sb", "b1_sb"))
        b0_sb = sb("b0_sb", [P, FB], F32)
        stats = sb("stats", [P, TT, 2, 6], F32)
        mv = sb("mv", [P, TT, 2], F32)
        var_eps = sb("var_eps", [P, TT], F32)
        rstd = sb("rstd", [P, TT], F32)
        minus_half = sb("minus_half", [P, TT], F32)
        row_max = sb("row_max", [P, HB], F32)
        row_sum = sb("row_sum", [P, HB], F32)
        row_inv = sb("row_inv", [P, HB], F32)

        pj = [psum(f"pj{b}") for b in range(3)]
        bank_t = [psum("bank_t0"), psum("bank_t1")]
        bank_s = psum("bank_s")
        bank_av = psum("bank_av", 2 * TOKENS)

        def as_f16(bank):
            return bank[:, 0:TOKENS // 2].bitcast(F16)

        def norm_banks(n, t):
            if n == 0 and t % 2:
                return bank_s[:], bank_av[:, 0:TOKENS]
            return bank_t[0][:], bank_t[1][:]

        x_landed = [sem(f"x_landed{n}") for n in range(2 * TT)]
        ctx_landed, bias_landed = sem("ctx_landed"), sem("bias_landed")
        landed = [sem(f"landed{s}") for s in range(SLOTS)]
        hi_done = [sem(f"hi_done{s}") for s in range(SLOTS)]
        ready = [sem(f"ready{s}") for s in range(SLOTS)]
        ctx_hi_done, ctx_ready = sem("ctx_hi_done"), sem("ctx_ready")
        products = sem("products")
        pj_taken = [sem(f"pj_taken{b}") for b in range(3)]
        t_full = [sem("t_full0"), sem("t_full1")]
        t_taken = [sem("t_taken0"), sem("t_taken1")]
        ln_full = [sem("ln_full0"), sem("ln_full1")]
        ln_hi = [sem("ln_hi0"), sem("ln_hi1")]
        ln_taken = [sem("ln_taken0"), sem("ln_taken1")]
        s_full, s_taken = sem("s_full"), sem("s_taken")
        av_full, av_taken = sem("av_full"), sem("av_taken")
        v_hi_done, pd_hi_done = sem("v_hi_done"), sem("pd_hi_done")
        at_hi_done = sem("at_hi_done")
        exp_done, probs_ready = sem("exp_done"), sem("probs_ready")
        soft_step, ln_step = sem("soft_step"), sem("ln_step")
        var_done, rstd_done, xn_done = sem("var_done"), sem("rstd_done"), sem("xn_done")
        gel_done, hidden_done = sem("gel_done"), sem("hidden_done")
        e_done, res_done = sem("e_done"), sem("res_done")
        const_set, const_done = sem("const_set"), sem("const_done")
        pd_cleared = sem("pd_cleared")
        stored = sem("stored")

        START = 1

        def wait(eng, s, value):
            if not (isinstance(value, int) and value <= 0):
                eng.wait_ge(s, value)

        def pair_tile(i, p, which):
            if STAGES[i][0] == "self":
                source = (sWq, sWk, sWv)[which]
            else:
                source = xWkv if which else xWq
            blocks = 2 * CKB if source is xWkv else KB
            return *pair_slot(i, p, which), source[bass.ds(p, 1)], blocks

        block = stack.enter_context(nc.Block())

        def after_pair(i, p, which):
            kind = STAGES[i][0]
            is_int = isinstance(p, int)
            if kind == "cross":
                if which == (2 if first_reversed(i, p) else 1):
                    return None
                if which == 0 and is_int and p == 0:
                    return pair_tile(i, 2, 0)
            s = pair_slot(i, p, which)[0]
            if is_int and (p == PAIRS - 1 or s == 2 and kind == "cross"):
                return o_tile(i, next(j for j in range(SLOTS) if o_slot(j) == s))
            return pair_tile(i, p + 1, which)

        def o_tile(i, j):
            kind = STAGES[i][0]
            return o_slot(j), o_slot_use(i, j), (xWo if kind == "cross" else sWo)[j:j + 1], KB

        def first_tile(i, s):
            if i == len(STAGES):
                return None
            if STAGES[i][0] == "ffn":
                return s, slot_uses_before(i, s), fW[s:s + 1], KB
            if s == 3:
                return None
            if STAGES[i][0] == "cross":
                return pair_tile(i, *((0, 0), (0, 1), (1, 0))[s])
            return pair_tile(i, 0, s)

        def after_o(i, j):
            if j < KB - SLOTS:
                return o_tile(i, j + SLOTS)
            return first_tile(i + 1, o_slot(j))

        def after_ffn(i, g, s):
            if isinstance(g, int) and g == FFN_GROUPS - 1:
                return first_tile(i + 1, s)
            return s, g + (slot_uses_before(i, s) + 1), fW[bass.ds(g * SLOTS + (SLOTS + s), 1)], KB

        @block.sync
        def _(sp):
            def load(tile):
                if tile is None:
                    return
                s, use, src, blocks = tile
                sp.wait_ge(ready[s], use + START)
                sp.dma_start(raw[:, s, 0:blocks, :], src.rearrange("a p k f -> (a p) k f")).then_inc(landed[s], 16)

            def load_x(n):
                sp.dma_start(res[:, n // TT, n % TT, :], x[n]).then_inc(x_landed[n], 16)

            for n in range(TT - 1):
                load_x(n)
            sp.dma_start(ctx_raw[:], ctxT[0]).then_inc(ctx_landed, 16)
            load(first_tile(0, 1))
            load_x(TT - 1)
            for s in (0, 2):
                load(first_tile(0, s))
            for n in range(TT, 2 * TT):
                load_x(n)
            for i in range(ATTN_STAGES):
                for w in range(3):
                    load(after_pair(i, 0, w))
                load(o_tile(i, 0))
                for w in range(3):
                    load(after_pair(i, 1, w))
                with sp.Fori(2, PAIRS - 1) as p:
                    for w in range(3):
                        load(after_pair(i, p, w))
                for w in range(3):
                    load(after_pair(i, PAIRS - 1, w))
                for j in range(KB):
                    if i == 0 and j == 0:
                        sp.wait_ge(ctx_ready, 1)
                        sp.dma_start(ctx_raw[:], ctxT[1]).then_inc(ctx_landed, 16)
                    load(after_o(i, j))
            for i in range(ATTN_STAGES, len(STAGES)):
                half = STAGES[i][1]

                def store(o, i=i, half=half):
                    sp.wait_ge(res_done, o + ((i - ATTN_STAGES) * KB + 1))
                    cols = bass.ds(o * P, P)
                    sp.dma_start(out[half, :, :, cols].rearrange("t p f -> p t f"), res[:, half, :, cols]).then_inc(stored, 16)

                for s in range(SLOTS):
                    load(after_ffn(i, 0, s))
                if i > ATTN_STAGES:
                    store_last()
                with sp.Fori(1, UP_GROUPS + 1) as g:
                    for s in range(SLOTS):
                        load(after_ffn(i, g, s))
                with sp.Fori(1, KB - 1) as o:
                    for s in range(SLOTS):
                        load(after_ffn(i, o + UP_GROUPS, s))
                    store(o - 1)
                for s in range(SLOTS):
                    load(after_ffn(i, FFN_GROUPS - 1, s))

                def store_last(store=store):
                    for o in range(KB - 2, KB):
                        store(o)
            store_last()
            sp.wait_ge(stored, 16 * 2 * KB)

        @block.scalar
        def _(act):
            for dst, src in [(bq_sb, bq), (bk_sb, bk), (bv_sb, bv), (bo_sb, bo), (b1_sb, b1), (b0_sb, b0)]:
                act.dma_start(dst[:], src).then_inc(bias_landed, 16)

            def round_tile(tile, freed):
                if tile is None:
                    return
                s, use, _, blocks = tile
                act.wait_ge(landed[s], 16 * (use + 1))
                wait(act, products, freed)
                nc.scalar.activation(w_hi[:, s, 0:blocks, :], raw[:, s, 0:blocks, :], ACT.Copy).then_inc(hi_done[s], 1)

            def round_ctx(n):
                act.wait_ge(ctx_landed, 16 * (n + 1))
                nc.scalar.activation(ctx_hi[:], ctx_raw[:], ACT.Copy).then_inc(ctx_hi_done, 1)

            def evacuate(dst, src, bias):
                if bias is None:
                    return nc.scalar.activation(dst, src, ACT.Copy)
                return nc.scalar.activation(dst, src, ACT.Identity, bias=bias)

            def take_pair(i, p, *between):
                biases = (bq_sb, bk_sb, bv_sb) if STAGES[i][0] == "self" else None

                def take(which, dst):
                    act.wait_ge(products, pair_product(i, p, which) + 1)
                    bias = biases[which][:, bass.ds(p, 1)] if biases else None
                    evacuate(dst[:], pj[which][:], bias).then_inc(pj_taken[which], 1)

                def next_tile(which):
                    round_tile(after_pair(i, p, which), pair_product(i, p, which) + 1)

                if first_reversed(i, p):
                    wait(act, t_full[1], pair_t_uses(i, 0))
                    take(2, vT)
                    take(1, kT)
                    next_tile(1)
                    take(0, qT)
                    next_tile(0)
                    return
                act.wait_ge(products, pair_product(i, p, 0) + 1)
                next_tile(0)
                for step in between:
                    step()
                wait(act, s_full, PAIRS * i + p)
                take(0, qT)
                take(1, kT)
                next_tile(1)
                if not isinstance(p, int) or p > 0:
                    act.wait_ge(t_full[0], pair_t_uses(i, p))
                take(2, vT)
                next_tile(2)

            def exp_pair(i, p):
                scale = HEAD_DIM ** -0.5 if STAGES[i][0] == "cross" else 1.0 / 4.0
                act.wait_ge(s_taken, PAIRS * i + p + 1 + START)
                nc.scalar.activation(probs[:], probs[:], ACT.Exp, scale=scale).then_inc(exp_done, 1)

            def values_hi(i, p):
                wait(act, av_full, PAIRS * i + p)
                act.wait_ge(t_full[0], pair_t_uses(i, p) + 1)
                nc.scalar.activation(v_hi[:].rearrange("p t d -> p (t d)"), bank_t[0][:], ACT.Copy).then_inc(v_hi_done, 1)

            def probs_hi(i, p):
                act.wait_ge(t_full[1], pair_t_uses(i, p) + 1)
                for b in range(2):
                    rows = slice(SEQ * b, SEQ * (b + 1))
                    nc.scalar.activation(pd_hi[rows, :, :, b, :], bank_t[1][rows].rearrange("p (t h q) -> p t h q", t=TT, h=2),
                                         ACT.Copy).then_inc(pd_hi_done, 1)

            def attn_hi(i, p):
                act.wait_ge(av_full, PAIRS * i + p + 1)
                for h in range(2):
                    head = slice(HEAD_DIM * h, HEAD_DIM * (h + 1))
                    nc.scalar.activation(at_hi[head, bass.ds(p, 1), :].rearrange("p a (t q) -> p (a t) q", t=TT),
                                         bank_av[head].rearrange("p (t h q) -> p t h q", t=TT, h=2)[:, :, h, :],
                                         ACT.Copy).then_inc(at_hi_done, 1)

            def normalised(n, t):
                kind, half = STAGES[n]
                ffn = kind == "ffn"
                for g in range(2):
                    act.wait_ge(ln_full[g], ln_tiles(n, t) + 1)
                    dst = xn_hi[:, half, KB // 2 * g:KB // 2 * (g + 1), bass.ds(t * P, P)]
                    bank = norm_banks(n, t)[g]
                    src = as_f16(bank) if ffn else bank
                    nc.scalar.activation(dst, src.rearrange("p (k t) -> p k t", t=P), ACT.Copy)\
                        .then_inc(ln_taken[g] if ffn else ln_hi[g], 1)

            round_ctx(0)
            normalised(0, 0)
            round_tile(first_tile(0, 1), 0)
            normalised(0, 1)
            round_tile(first_tile(0, 0), 0)
            normalised(0, 2)
            normalised(0, 3)
            round_tile(first_tile(0, 2), 0)
            for i in range(ATTN_STAGES):
                if STAGES[i][0] == "self":
                    act.wait_ge(bias_landed, 16 * 6)
                take_pair(i, 0)
                round_tile(o_tile(i, 0), products_before(i))

                def pair_step(p, out_before=True, norm=False):
                    if norm:
                        normalised(i + 1, p - 2)
                    if out_before:
                        attn_hi(i, p - 2)
                    values_hi(i, p - 1)
                    exp_pair(i, p - 1)
                    take_pair(i, p, lambda: probs_hi(i, p - 1))

                if i == 0:
                    act.wait_ge(pd_cleared, 2)
                pair_step(1, out_before=False)
                with act.Fori(2, 2 + TT) as p:
                    pair_step(p, norm=True)
                for p in range(2 + TT, PAIRS):
                    pair_step(p)
                attn_hi(i, PAIRS - 2)
                values_hi(i, PAIRS - 1)
                exp_pair(i, PAIRS - 1)
                probs_hi(i, PAIRS - 1)
                attn_hi(i, PAIRS - 1)
                for j in range(KB):
                    b = O_BANKS[j]
                    act.wait_ge(products, o_product(i, j) + 1)
                    act.wait_ge(t_full[j % 2], o_t_uses(i, j))
                    evacuate(o_T[j % 2][:], pj[b][:], bo_sb[:, j:j + 1] if STAGES[i][0] == "self" else None).then_inc(pj_taken[b], 1)
                    if i == 0 and j == KB // 2:
                        round_ctx(1)
                    round_tile(after_o(i, j), o_product(i, j) + 1)
            for i in range(ATTN_STAGES, len(STAGES)):
                before = products_before(i)
                gelus = (i - ATTN_STAGES) * FB

                def gelu(j, s):
                    act.wait_ge(products, before + j + 1)
                    wait(act, hidden_done, gelus + j - 1)
                    nc.scalar.activation(gel[:, s % 2, :], pj[s % 2][:], ACT.Gelu, bias=b0_sb[:, bass.ds(j, 1)]).then_inc(gel_done, 1)

                def up_group(g, norm=False):
                    for s in range(SLOTS):
                        gelu(g * SLOTS + s, s)
                        if norm:
                            normalised(i + 1, s)
                        round_tile(after_ffn(i, g, s), g * SLOTS + (before + s + 1))

                up_group(0)
                if i == ATTN_STAGES:
                    up_group(1, norm=True)
                with act.Fori(2 if i == ATTN_STAGES else 1, UP_GROUPS) as g:
                    up_group(g)

                def take_out(o, b, earlier):
                    for s in range(SLOTS):
                        freed = o * SLOTS + (before + FB + s + 1)
                        act.wait_ge(products, freed)
                        if s == SLOTS - 1:
                            act.wait_ge(t_full[b], earlier + ffn_t_uses(i, 0))
                            nc.scalar.activation(e_T[:, b, :], pj[b][:], ACT.Identity, bias=b1_sb[:, bass.ds(o, 1)]).then_inc(e_done, 1)
                        round_tile(after_ffn(i, o + UP_GROUPS, s), freed)

                with act.Fori(0, KB // 2 - 1) as g:
                    for b in range(2):
                        take_out(g * 2 + b, b, g)
                for o in range(KB - 2, KB):
                    take_out(o, o % 2, o // 2)

        def lower(engine, eng, tile):
            if tile is None:
                return
            s, use, _, blocks = tile
            eng.wait_ge(hi_done[s], use + 1)
            engine.tensor_tensor(w_lo[:, s, 0:blocks, :], raw[:, s, 0:blocks, :], w_hi[:, s, 0:blocks, :].bitcast(F32),
                                 ALU.subtract).then_inc(ready[s], 1)

        @block.gpsimd
        def _(pool):
            nc.gpsimd.memset(minus_half[:], -0.5).then_inc(const_set, 1)
            nc.gpsimd.memset(ident[:], 0.0).then_inc(const_set, 1)
            nc.gpsimd.memset(mask[:], 0.0).then_inc(const_set, 1)
            pool.wait_ge(const_set, 3)
            nc.gpsimd.affine_select(out=ident[:], in_=ident[:], compare_op=ALU.not_equal, fill=1.0, base=0,
                                    pattern=[[-1, P]], channel_multiplier=1).then_inc(const_set, 1)
            pool.wait_ge(const_set, 4)
            nc.gpsimd.tensor_copy(ident16[:], ident[:]).then_inc(const_done, 1)

            def lower_ctx(n):
                pool.wait_ge(ctx_hi_done, n + 1)
                nc.gpsimd.tensor_tensor(ctx_lo[:], ctx_raw[:], ctx_hi[:].bitcast(F32), ALU.subtract).then_inc(ctx_ready, 1)

            def inverse_root(n):
                pool.wait_ge(var_done, TT + n)
                nc.gpsimd.tensor_tensor(rstd[:], var_eps[:], minus_half[:], ALU.pow).then_inc(rstd_done, 1)

            for t in range(TT):
                if t == TT - 1:
                    lower_ctx(0)
                    lower(nc.gpsimd, pool, first_tile(0, 1))
                pool.wait_ge(var_done, t + 1)
                nc.gpsimd.tensor_tensor(rstd[:, t:t + 1], var_eps[:, t:t + 1], minus_half[:, t:t + 1], ALU.pow).then_inc(rstd_done, 1)
            for s in (0, 2):
                lower(nc.gpsimd, pool, first_tile(0, s))
            pool.wait_ge(ready[2], 1 + START)
            for h in range(2):
                part = slice(SEQ * h, SEQ * (h + 1))
                pool.wait_ge(const_done, 1 + h)
                nc.gpsimd.affine_select(out=mask[part], in_=mask[part], compare_op=ALU.is_ge, fill=MASKED, base=0,
                                        pattern=[[-1, SEQ]], channel_multiplier=1).then_inc(const_done, 1)
            pool.wait_ge(const_done, 3)
            nc.gpsimd.memset(pd_hi[:].bitcast(F32), 0.0).then_inc(pd_cleared, 1)
            nc.gpsimd.memset(pd_lo[:].bitcast(F32), 0.0).then_inc(pd_cleared, 1)
            for i in range(ATTN_STAGES):
                pool_tiles = range(1, 3) if STAGES[i][0] == "cross" else range(3)
                if 0 in pool_tiles:
                    lower(nc.gpsimd, pool, after_pair(i, 0, 0))
                inverse_root(i + 1)
                for w in range(1, 3):
                    lower(nc.gpsimd, pool, after_pair(i, 0, w))
                lower(nc.gpsimd, pool, o_tile(i, 0))
                for w in pool_tiles:
                    lower(nc.gpsimd, pool, after_pair(i, 1, w))
                with pool.Fori(2, PAIRS - 1) as p:
                    for w in pool_tiles:
                        lower(nc.gpsimd, pool, after_pair(i, p, w))
                for w in pool_tiles:
                    lower(nc.gpsimd, pool, after_pair(i, PAIRS - 1, w))
                for j in range(KB):
                    if i == 0 and j == KB // 2:
                        lower_ctx(1)
                    lower(nc.gpsimd, pool, after_o(i, j))
            lower(nc.gpsimd, pool, after_ffn(ATTN_STAGES, 0, 0))
            inverse_root(ATTN_STAGES + 1)
            for s in range(1, SLOTS):
                lower(nc.gpsimd, pool, after_ffn(ATTN_STAGES, 0, s))

        @block.vector
        def _(dve):
            ln_steps = 0

            def ordered(instruction):
                nonlocal ln_steps
                instruction.then_inc(ln_step, 1)
                ln_steps += 1
                dve.wait_ge(ln_step, ln_steps)

            def statistics(n, tiles):
                half = STAGES[n][1]
                for t in tiles:
                    if n < 2:
                        dve.wait_ge(x_landed[half * TT + t], 16)
                    for g in range(2):
                        last = nc.vector.bn_stats(stats[:, t, g, :], res[:, half, t, g * HIDDEN // 2:(g + 1) * HIDDEN // 2])
                ordered(last)
                for t in tiles:
                    last = nc.vector.bn_aggr(mv[:, t, :], stats[:, t, :, :].rearrange("p g s -> p (g s)"))
                ordered(last)
                cols = slice(tiles[0], tiles[-1] + 1)
                nc.vector.tensor_scalar(var_eps[:, cols], mv[:, cols, 1], LN_EPS, None, ALU.add).then_inc(var_done, 1)

            def scale_tile(n, t, buffer):
                dve.wait_ge(rstd_done, t + 1 if n == 0 else TT + n)
                here = bass.ds(t, 1)
                nc.vector.tensor_scalar(buffer, res[:, STAGES[n][1], here, :].rearrange("p a f -> p (a f)"),
                                        mv[:, here, 0], rstd[:, here], ALU.subtract, ALU.mult).then_inc(xn_done, 1)

            def norm_lo(n, t):
                kind, half = STAGES[n]
                if kind == "ffn":
                    return
                for g in range(2):
                    dve.wait_ge(ln_hi[g], ln_tiles(n, t) + 1)
                    cols = (slice(None), slice(KB // 2 * g, KB // 2 * (g + 1)), bass.ds(t * P, P))
                    nc.vector.tensor_tensor(xn_lo[half][cols], norm_banks(n, t)[g].rearrange("p (k t) -> p k t", t=P),
                                            xn_hi[:, half][cols].bitcast(F32), ALU.subtract).then_inc(ln_taken[g], 1)

            def by_batch(ap):
                return ap.unsqueeze(2).to_broadcast([P, HB, SEQ])

            def softmax(i, p, *between):
                self_attn = STAGES[i][0] == "self"
                n = PAIRS * i + p
                t_uses = pair_t_uses(i, p)
                scores = bank_s[:].rearrange("p (b k) -> p b k", b=HB)
                dve.wait_ge(s_full, n + 1)
                dve.wait_ge(t_full[1], t_uses)
                if not self_attn:
                    if isinstance(n, int) and n == 0:
                        dve.wait_ge(const_done, 3)
                    nc.vector.tensor_tensor(probs[:], scores, mask[:].unsqueeze(1).to_broadcast([P, HB, SEQ]),
                                            ALU.add).then_inc(soft_step, 1)
                    dve.wait_ge(soft_step, soft_steps(i, p, 1))
                    scores = probs[:]
                k = 0 if self_attn else 1
                nc.vector.tensor_reduce(row_max[:], scores, AX.X, ALU.max).then_inc(soft_step, 1)
                dve.wait_ge(soft_step, soft_steps(i, p, k + 1))
                nc.vector.tensor_tensor(probs[:], scores, by_batch(row_max[:]), ALU.subtract).then_inc(s_taken, 1)
                for step in between:
                    step()
                dve.wait_ge(exp_done, n + 1)
                nc.vector.tensor_reduce(row_sum[:], probs[:], AX.X, ALU.add).then_inc(soft_step, 1)
                dve.wait_ge(soft_step, soft_steps(i, p, k + 2))
                nc.vector.reciprocal(row_inv[:], row_sum[:]).then_inc(soft_step, 1)
                dve.wait_ge(soft_step, soft_steps(i, p, k + 3))
                nc.vector.tensor_tensor(probs[:], probs[:], by_batch(row_inv[:]), ALU.mult).then_inc(probs_ready, 1)

            def values_lo(i, p):
                dve.wait_ge(v_hi_done, PAIRS * i + p + 1)
                nc.vector.tensor_tensor(v_lo[:].rearrange("p t d -> p (t d)"), bank_t[0][:],
                                        v_hi[:].rearrange("p t d -> p (t d)").bitcast(F32), ALU.subtract).then_inc(t_taken[0], 1)

            def probs_lo(i, p):
                for b in range(2):
                    rows = slice(SEQ * b, SEQ * (b + 1))
                    dve.wait_ge(pd_hi_done, (PAIRS * i + p) * 2 + (b + 1))
                    last = nc.vector.tensor_tensor(pd_lo[rows, :, :, b, :],
                                                   bank_t[1][rows].rearrange("p (t h q) -> p t h q", t=TT, h=2),
                                                   pd_hi[rows, :, :, b, :].bitcast(F32), ALU.subtract)
                last.then_inc(t_taken[1], 1)

            def attn_lo(i, p):
                at = bass.ds(p, 1)
                for h in range(2):
                    head = slice(HEAD_DIM * h, HEAD_DIM * (h + 1))
                    dve.wait_ge(at_hi_done, (PAIRS * i + p) * 2 + (h + 1))
                    last = nc.vector.tensor_tensor(at_lo[head, at, :].rearrange("p a (t q) -> p (a t) q", t=TT),
                                                   bank_av[head].rearrange("p (t h q) -> p t h q", t=TT, h=2)[:, :, h, :],
                                                   at_hi[head, at, :].rearrange("p a (t q) -> p (a t) q", t=TT).bitcast(F32),
                                                   ALU.subtract)
                last.then_inc(av_taken, 1)

            def soft_steps(i, p, k):
                per = {"cross": 4, "self": 3}
                before = sum(per[STAGES[n][0]] * PAIRS for n in range(i))
                return p * per[STAGES[i][0]] + (before + k)

            statistics(0, [0])
            statistics(0, [1])
            scale_tile(0, 0, xn[:, 0, :])
            statistics(0, [2])
            scale_tile(0, 1, xn[:, 1, :])
            norm_lo(0, 0)
            statistics(0, [3])
            for t in range(2, TT):
                dve.wait_ge(ln_full[1], t - 1)
                scale_tile(0, t, xn[:, t % 2, :])
            for t in range(1, TT):
                norm_lo(0, t)
            for i in range(ATTN_STAGES):
                half = STAGES[i][1]
                statistics(i + 1, range(TT))
                one_tile = xn[:, 0, 0:HIDDEN // 2].bitcast(F16) if STAGES[i + 1][0] == "ffn" else xn[:, 0, :]

                cross = STAGES[i][0] == "cross"
                if cross:
                    lower(nc.vector, dve, after_pair(i, 0, 0))

                def attend(p, scale_next=False, norm=False):
                    if norm:
                        norm_lo(i + 1, p - 1)
                    softmax(i, p, lambda: values_lo(i, p))
                    if not isinstance(p, int) or p > 0:
                        attn_lo(i, p - 1)
                    if scale_next:
                        scale_tile(i + 1, p, one_tile)
                    if cross and not (isinstance(p, int) and p == PAIRS - 1):
                        lower(nc.vector, dve, after_pair(i, p + 1, 0))
                    probs_lo(i, p)

                if i == 0:
                    dve.wait_ge(pd_cleared, 2)
                attend(0, scale_next=True)
                with dve.Fori(1, TT) as p:
                    attend(p, scale_next=True, norm=True)
                attend(TT, norm=True)
                for p in range(TT + 1, PAIRS):
                    attend(p)
                attn_lo(i, PAIRS - 1)
                for j in range(KB):
                    g = j % 2
                    dve.wait_ge(t_full[g], o_t_uses(i, j) + 1)
                    here = res[:, half, :, j * P:(j + 1) * P]
                    nc.vector.tensor_tensor(here, here, bank_t[g][:].rearrange("p (t f) -> p t f", t=TT),
                                            ALU.add).then_inc(t_taken[g], 1)
                for g in range(2):
                    dve.wait_ge(t_taken[g], o_t_uses(i, KB - 1) + 1)
            for i in range(ATTN_STAGES, len(STAGES)):
                half = STAGES[i][1]
                gelus = (i - ATTN_STAGES) * FB

                def copy_hidden(j, s):
                    dve.wait_ge(gel_done, gelus + j + 1)
                    nc.vector.tensor_copy(hidden[:, bass.ds(j, 1), :].rearrange("p a t -> p (a t)"), gel[:, s % 2, :]).then_inc(hidden_done, 1)

                if i == ATTN_STAGES:
                    statistics(i + 1, range(TT))
                for s in range(SLOTS):
                    copy_hidden(s, s)
                    if i == ATTN_STAGES and s == 1:
                        for t in range(TT):
                            scale_tile(i + 1, t, ffn_tiles[:, t, :])
                    if i > ATTN_STAGES:
                        lower(nc.vector, dve, after_ffn(i, 0, s))
                with dve.Fori(1, UP_GROUPS) as g:
                    for s in range(SLOTS):
                        copy_hidden(g * SLOTS + s, s)
                        lower(nc.vector, dve, after_ffn(i, g, s))

                def add_out(o, b, earlier):
                    dve.wait_ge(t_full[b], earlier + (ffn_t_uses(i, 0) + 1))
                    here = res[:, half, :, bass.ds(o * P, P)]
                    nc.vector.tensor_tensor(here, here, as_f16(bank_t[b]).rearrange("p (t f) -> p t f", t=TT),
                                            ALU.add).then_inc(res_done, 1)

                def out_step(o, before=None):
                    for s in range(SLOTS):
                        lower(nc.vector, dve, after_ffn(i, o + UP_GROUPS, s))
                        if s == 1 and before:
                            add_out(*before)

                out_step(0)
                out_step(1, (0, 0, 0))
                with dve.Fori(1, KB // 2 - 1) as g:
                    out_step(g * 2, (g * 2 - 1, 1, g - 1))
                    out_step(g * 2 + 1, (g * 2, 0, g))
                for o in range(KB - 2, KB):
                    out_step(o, (o - 1, (o - 1) % 2, (o - 1) // 2))
                add_out(KB - 1, 1, KB // 2 - 1)

        @block.tensor
        def _(pe):
            for s in [*ready, *pj_taken, s_taken, av_taken]:
                pe.sem_inc(s, START)
            pe.wait_ge(const_done, 1)

            def accumulate(bank, terms, start=True, stop=True):
                for n, (lhs, rhs) in enumerate(terms):
                    last = nc.tensor.matmul(bank[:], lhs, rhs, start=start and n == 0, stop=stop and n == len(terms) - 1)
                return last

            def exact(s, blocks, hi, lo):
                for n, k in enumerate(blocks):
                    yield w_hi[:, s, k, :], hi[:, n, :]
                    yield w_hi[:, s, k, :], lo[:, n, :]
                    yield w_lo[:, s, k, :], hi[:, n, :]

            def tile_ready(s, use):
                pe.wait_ge(ready[s], use + 1 + START)

            def project(i, p, which, *between):
                kind, half = STAGES[i]
                pe.wait_ge(pj_taken[which], bank_uses_before(i, which) + p + START)
                tile_ready(*pair_slot(i, p, which))
                s = pair_slot(i, p, which)[0]
                if kind == "cross" and which:
                    blocks, hi, lo = range(CKB * (which - 1), CKB * which), ctx_hi, ctx_lo
                else:
                    blocks, hi, lo = range(KB), xn_hi[:, half], xn_lo[half]
                cuts = [0, *(block for block, _ in between), len(blocks)]
                for n, (first, end) in enumerate(zip(cuts, cuts[1:])):
                    if n:
                        between[n - 1][1]()
                    if first < end:
                        terms = list(exact(s, blocks[first:end], hi[:, first:end], lo[:, first:end]))
                        last = accumulate(pj[which], terms, start=first == 0, stop=end == len(blocks))
                last.then_inc(products, 1)

            def scores_inputs(i, p):
                n = PAIRS * i + p
                pe.wait_ge(pj_taken[0], bank_uses_before(i, 0) + p + 1 + START)
                pe.wait_ge(pj_taken[1], bank_uses_before(i, 1) + p + 1 + START)
                pe.wait_ge(s_taken, n + START)

            def scores():
                for b in range(HB):
                    cols = slice(SEQ * b, SEQ * (b + 1))
                    for h in range(2):
                        head = slice(HEAD_DIM * h, HEAD_DIM * (h + 1))
                        last = nc.tensor.matmul(bank_s[head, cols], qT[head, cols], kT[head, cols], start=True, stop=True)
                last.then_inc(s_full, 1)

            def transpose_v(i, p, normed=False):
                if normed:
                    for g in range(2):
                        pe.wait_ge(ln_taken[g], ln_tiles(i + 1, p))
                pe.wait_ge(pj_taken[2], bank_uses_before(i, 2) + p + 1 + START)
                pe.wait_ge(t_taken[0], pair_t_uses(i, p))
                for t in range(TT):
                    cols = slice(t * P, (t + 1) * P)
                    last = nc.tensor.transpose(bank_t[0][:, cols], vT[:, cols], ident[:])
                last.then_inc(t_full[0], 1)

            def transpose_probs(i, p):
                pe.wait_ge(probs_ready, PAIRS * i + p + 1)
                pe.wait_ge(t_taken[1], pair_t_uses(i, p))
                flat = probs[:].rearrange("p b k -> p (b k)")
                for t in range(TT):
                    cols = slice(t * P, (t + 1) * P)
                    last = nc.tensor.transpose(bank_t[1][:, cols], flat[:, cols], ident[:])
                last.then_inc(t_full[1], 1)

            def weigh_values(i, p):
                pe.wait_ge(t_taken[0], pair_t_uses(i, p) + 1)
                pe.wait_ge(t_taken[1], pair_t_uses(i, p) + 1)
                pe.wait_ge(av_taken, PAIRS * i + p + START)
                for t in range(TT):
                    terms = [(v[:, t, :], pd[:, t].rearrange("p h b q -> p (h b q)"))
                             for v, pd in ((v_hi, pd_hi), (v_hi, pd_lo), (v_lo, pd_hi))]
                    last = accumulate(bank_av[:, t * 2 * P:(t + 1) * 2 * P], terms)
                last.then_inc(av_full, 1)

            def normalised(n, t, tile, banks=(0, 1)):
                ffn = STAGES[n][0] == "ffn"
                pe.wait_ge(xn_done, ln_tiles(n, t) + 1)
                for g in banks:
                    for k in range(KB // 2):
                        cols = slice((KB // 2 * g + k) * P, (KB // 2 * g + k + 1) * P)
                        bank = norm_banks(n, t)[g]
                        dst = as_f16(bank) if ffn else bank
                        if k == 0:
                            wait(pe, ln_taken[g], t - 1 if n == 0 else ln_tiles(n, t))
                            if 0 < n <= ATTN_STAGES:
                                pe.wait_ge(t_taken[g], pair_t_uses(n - 1, t) + 1)
                            elif n:
                                pe.wait_ge(t_taken[g], ffn_t_uses(ATTN_STAGES, 0))
                        last = nc.tensor.transpose(dst[:, k * P:(k + 1) * P], tile[:, cols], (ident16 if ffn else ident)[:])
                    last.then_inc(ln_full[g], 1)

            def xn_is_ready(i, g):
                pe.wait_ge(ln_taken[g], ln_tiles(i + 1, 0))

            for t in range(2):
                normalised(0, t, xn[:, t % 2, :])
            finish = None
            for i in range(ATTN_STAGES):
                kind, half = STAGES[i]
                rest = [(1 if kind == "cross" else 2, finish)] if finish else []
                upper_half = (KB // 2, lambda: xn_is_ready(i, 1))
                if kind == "cross":
                    pe.wait_ge(ctx_ready, i + 1)
                    project(i, 0, 2, *rest)
                    if i == 0:
                        for t in range(2, TT):
                            normalised(0, t, xn[:, t % 2, :])
                    project(i, 0, 1)
                    xn_is_ready(i, 0)
                    project(i, 0, 0, upper_half)
                else:
                    xn_is_ready(i, 0)
                    project(i, 0, 0, *rest, upper_half)
                    project(i, 0, 1)
                    project(i, 0, 2)
                one_tile = xn[:, 0, 0:HIDDEN // 2].bitcast(F16) if STAGES[i + 1][0] == "ffn" else xn[:, 0, :]
                probs_at = CKB // 2 if kind == "cross" else KB // 2

                def pair_step(p, values_before=True, norm=False):
                    if norm:
                        normalised(i + 1, p - 2, one_tile, banks=[0])

                    def attend_inputs():
                        scores_inputs(i, p - 1)
                        if norm:
                            normalised(i + 1, p - 2, one_tile, banks=[1])

                    def attend():
                        scores()
                        if values_before:
                            weigh_values(i, p - 2)

                    project(i, p, 0, (1, attend_inputs), (2, attend), (3, lambda: transpose_v(i, p - 1, norm)))
                    project(i, p, 1, (probs_at, lambda: transpose_probs(i, p - 1)))
                    project(i, p, 2)

                pair_step(1, values_before=False)
                if i == 0:
                    pe.wait_ge(pd_cleared, 2)
                with pe.Fori(2, 2 + TT) as p:
                    pair_step(p, norm=True)
                with pe.Fori(2 + TT, PAIRS) as p:
                    pair_step(p)

                last = PAIRS - 1

                def o_part(j, blocks, start, stop):
                    s, b = o_slot(j), O_BANKS[j]
                    if start:
                        pe.wait_ge(pj_taken[b], bank_uses_before(i, b) + PAIRS + j // 3 + START)
                        tile_ready(s, o_slot_use(i, j))
                    terms = list(exact(s, blocks, at_hi[:, blocks.start:blocks.stop], at_lo[:, blocks.start:blocks.stop]))
                    return accumulate(pj[b], terms, start, stop)

                def open_tiles(*parts):
                    for j, first, end in parts:
                        o_part(j, range(first, end), first == 0, False)

                opened = (KB - 1, KB - 3, KB // 2)
                pe.wait_ge(av_taken, PAIRS * i + last - 1 + START)
                open_tiles((0, 0, 1))
                scores_inputs(i, last)
                open_tiles((0, 1, 2))
                scores()
                weigh_values(i, last - 1)
                transpose_v(i, last)
                open_tiles((0, 2, 6), (1, 0, 2))
                transpose_probs(i, last)
                open_tiles((1, 2, opened[1]))
                pe.wait_ge(av_taken, PAIRS * i + last + START)
                open_tiles((0, 6, opened[0]))
                weigh_values(i, last)
                open_tiles((2, 0, opened[2]))
                pe.wait_ge(av_taken, PAIRS * i + last + 1 + START)

                def transpose_o(j, i=i):
                    g, b = j % 2, O_BANKS[j]
                    pe.wait_ge(pj_taken[b], bank_uses_before(i, b) + PAIRS + j // 3 + 1 + START)
                    pe.wait_ge(t_taken[g], o_t_uses(i, j))
                    for t in range(TT):
                        cols = slice(t * P, (t + 1) * P)
                        done = nc.tensor.transpose(bank_t[g][:, cols], o_T[g][:, cols], ident[:])
                    done.then_inc(t_full[g], 1)

                for j in range(KB):
                    if j < 3:
                        o_part(j, range(opened[j], KB), False, True).then_inc(products, 1)
                    else:
                        o_part(j, range(0, KB), True, True).then_inc(products, 1)
                    if j:
                        transpose_o(j - 1)

                def finish(transpose_o=transpose_o):
                    transpose_o(KB - 1)

            for i in range(ATTN_STAGES, len(STAGES)):
                half = STAGES[i][1]
                n = i - ATTN_STAGES
                bank_base = bank_uses_before(i, 0)
                for g in range(2):
                    xn_is_ready(i, g)

                def ffn_up(g, after=None):
                    for s in range(SLOTS):
                        b = s % 2
                        if s >= 2:
                            pe.wait_ge(gel_done, g * SLOTS + (n * FB + s - 1))
                        elif isinstance(g, int) and g == 0:
                            if n == 0:
                                pe.wait_ge(pj_taken[b], bank_base + START)
                            else:
                                pe.wait_ge(e_done, n * KB - 1 + s)
                        else:
                            pe.wait_ge(gel_done, g * SLOTS + (n * FB + s - 1))
                        tile_ready(s, slot_uses_before(i, s) + g)
                        terms = [(w[:, s, k, :], xn_hi[:, half, k, :]) for k in range(KB) for w in (w_hi, w_lo)]
                        accumulate(pj[b], terms).then_inc(products, 1)
                        if after:
                            after(s)

                def ffn_down(o, b, before=None):
                    if isinstance(o, int) and o < 2:
                        pe.wait_ge(gel_done, n * FB + FB - 1 + o)
                    else:
                        pe.wait_ge(e_done, o + (n * KB - 1))
                    for s in range(SLOTS):
                        if isinstance(o, int) and o == 0:
                            pe.wait_ge(hidden_done, n * FB + KB * (s + 1))
                        tile_ready(s, o + (slot_uses_before(i, s) + UP_GROUPS))
                        terms = [(w[:, s, k, :], hidden[:, s * KB + k, :]) for k in range(KB) for w in (w_hi, w_lo)]
                        accumulate(pj[b], terms, start=s == 0, stop=s == SLOTS - 1).then_inc(products, 1)
                        if s == 0 and before is not None:
                            transpose_e(before, 1 - b)

                def transpose_e(o, b, n=n, i=i):
                    pe.wait_ge(e_done, o + (n * KB + 1))
                    if isinstance(o, int) and n * KB + o < 2:
                        pe.wait_ge(ln_taken[b], ln_tiles(i + 2, 0))
                    else:
                        pe.wait_ge(res_done, o + (n * KB - 1))
                    bank16 = as_f16(bank_t[b])
                    for t in range(TT):
                        cols = slice(t * P, (t + 1) * P)
                        done = nc.tensor.transpose(bank16[:, cols], e_T[:, b, cols], ident16[:])
                    done.then_inc(t_full[b], 1)

                if i == ATTN_STAGES:
                    ffn_up(0, lambda s: s == 0 and finish())
                    ffn_up(1, lambda s: normalised(i + 1, s, ffn_tiles[:, s, :]))
                else:
                    ffn_up(0, lambda s: s == 0 and finish())
                with pe.Fori(2 if i == ATTN_STAGES else 1, UP_GROUPS) as g:
                    ffn_up(g)
                ffn_down(0, 0)
                ffn_down(1, 1, 0)
                with pe.Fori(1, KB // 2) as g:
                    ffn_down(g * 2, 0, g * 2 - 1)
                    ffn_down(g * 2 + 1, 1, g * 2)

                def finish(transpose_e=transpose_e):
                    transpose_e(KB - 1, 1)
            finish()


def weight_tiles(w, out_blocks, in_blocks):
    return w.reshape(out_blocks, P, in_blocks, P).transpose(0, 3, 2, 1)


def kernel(x, ctx_512, L0_xattn_Wq, L0_xattn_Wkv_expand, L0_xattn_Wout, L0_attn_Wq, L0_attn_bq, L0_attn_Wk,
           L0_attn_bk, L0_attn_Wv, L0_attn_bv, L0_attn_Wo, L0_attn_bo, L0_ffn_W0, L0_ffn_bias0, L0_ffn_W1,
           L0_ffn_bias1):
    from concourse import bacc
    from concourse.bass_utils import run_bass_kernel_spmd

    def columns(b):
        return np.asarray(b).reshape(-1, P).T

    wkv = np.asarray(L0_xattn_Wkv_expand)
    kv = [weight_tiles(wkv[n * HIDDEN:(n + 1) * HIDDEN], PAIRS, CKB) for n in range(2)]
    ctx = np.asarray(ctx_512)[:, :SEQ, :].reshape(2, TOKENS, CKB, P).transpose(0, 3, 2, 1)
    w1 = np.asarray(L0_ffn_W1).reshape(KB, P, FKB, KB, P).transpose(0, 2, 4, 3, 1).reshape(KB * FKB, P, KB, P)
    ins = {
        "x": np.asarray(x).reshape(2 * TT, P, HIDDEN),
        "ctxT": ctx,
        "xWq": weight_tiles(np.asarray(L0_xattn_Wq), PAIRS, KB),
        "xWkv": np.concatenate(kv, axis=2),
        "xWo": weight_tiles(np.asarray(L0_xattn_Wout), KB, KB),
        "sWq": weight_tiles(np.asarray(L0_attn_Wq).T, PAIRS, KB),
        "sWk": weight_tiles(np.asarray(L0_attn_Wk).T, PAIRS, KB),
        "sWv": weight_tiles(np.asarray(L0_attn_Wv).T, PAIRS, KB),
        "sWo": weight_tiles(np.asarray(L0_attn_Wo).T, KB, KB),
        "fW": np.concatenate([weight_tiles(np.asarray(L0_ffn_W0), FB, KB), w1], axis=0),
        "bq": columns(L0_attn_bq), "bk": columns(L0_attn_bk), "bv": columns(L0_attn_bv),
        "bo": columns(L0_attn_bo), "b0": columns(L0_ffn_bias0), "b1": columns(L0_ffn_bias1),
    }
    ins = {f"in_{n}": np.ascontiguousarray(a) for n, a in ins.items()}
    nc = bacc.Bacc("TRN2", target_bir_lowering=False, num_devices=1, dynamic_dma_scratch_size=1024)
    args = [nc.dram_tensor(n, a.shape, F32, kind="ExternalInput").ap() for n, a in ins.items()]
    out = nc.dram_tensor("out", (2, TT, P, HIDDEN), F32, kind="ExternalOutput").ap()
    build(nc, *args, out)
    result = run_bass_kernel_spmd(nc, [ins], core_ids=[0])
    return result.results[0]["out"].reshape(BATCHES, SEQ, HIDDEN)
```
